# Optimizing a Trainium2 kernel written in Bass

```python
import numpy as np
import jax
import jax.numpy as jnp

def _softmax(x, axis=-1):
    return jax.nn.softmax(x, axis=axis)
def _gelu(x):
    return jax.nn.gelu(x, approximate=True)
def _silu(x):
    return jax.nn.silu(x)
def _sigmoid(x):
    return jax.nn.sigmoid(x)
def _layernorm(x, axis=-1, eps=1e-5):
    m = jnp.mean(x, axis=axis, keepdims=True)
    v = jnp.var(x, axis=axis, keepdims=True)
    return (x - m) / jnp.sqrt(v + eps)
def _scatter_add(tgt, idx, src, axis=0):
    return tgt.at[idx].add(src)
def _segment_sum(src, seg, n):
    return jax.ops.segment_sum(src, seg, n)

kernel_name = 'mk_conv_seq_d1_conv_nchw512_a78a9c'

def setup_inputs(seed: int = 0):
    np.random.seed(seed)
    _w = jnp.asarray
    def _rec_inputs():
        import jax
        import jax.numpy as jnp
        _gk = jax.random.key(seed)
        x = -0.000125 + 0.9999 * jax.random.normal(jax.random.fold_in(_gk, 1), (4, 512, 128, 128), jnp.float32)
        return x
    x = _rec_inputs()
    def _L0_conv_setup():
        import jax, jax.numpy as jnp
        import numpy as np
        B, C, H, W = (4, 512, 128, 128)
        CQ = C // 8
        key = jax.random.key(seed)
        ks = jax.random.split(key, 8)
        s = 0.05
        return {'x': jax.random.normal(ks[0], (B, C, H, W), jnp.float32), 'Wq': jax.random.normal(ks[1], (CQ, C), jnp.float32) * s, 'bq': jax.random.normal(ks[2], (CQ,), jnp.float32) * s, 'Wk': jax.random.normal(ks[3], (CQ, C), jnp.float32) * s, 'bk': jax.random.normal(ks[4], (CQ,), jnp.float32) * s, 'Wv': jax.random.normal(ks[5], (C, C), jnp.float32) * s, 'bv': jax.random.normal(ks[6], (C,), jnp.float32) * s, 'gamma': jax.random.uniform(ks[7], (1,), jnp.float32)}
    _L0_conv_all = _L0_conv_setup()
    _L0_conv_in = {k: v for k, v in _L0_conv_all.items() if k in ('Wq', 'bq', 'Wk', 'bk', 'Wv', 'bv', 'gamma', )}
    del _L0_conv_all

    return {
        "x": x,
        "L0_conv_Wq": _L0_conv_in["Wq"],
        "L0_conv_bq": _L0_conv_in["bq"],
        "L0_conv_Wk": _L0_conv_in["Wk"],
        "L0_conv_bk": _L0_conv_in["bk"],
        "L0_conv_Wv": _L0_conv_in["Wv"],
        "L0_conv_bv": _L0_conv_in["bv"],
        "L0_conv_gamma": _L0_conv_in["gamma"],
    }

def reference(x, L0_conv_Wq, L0_conv_bq, L0_conv_Wk, L0_conv_bk, L0_conv_Wv, L0_conv_bv, L0_conv_gamma):
    import jax
    import jax.numpy as jnp
    def _L0_conv_ref(x, Wq, bq, Wk, bk, Wv, bv, gamma):
        import jax, jax.numpy as jnp
        import numpy as np
        B, C, H, W = (4, 512, 128, 128)
        CQ = C // 8
        q = jnp.einsum('oc,bchw->bohw', Wq, x) + bq[None, :, None, None]
        k = jnp.einsum('oc,bchw->bohw', Wk, x) + bk[None, :, None, None]
        v = jnp.einsum('oc,bchw->bohw', Wv, x) + bv[None, :, None, None]
        h = x.shape[2]
        energy_H = jnp.einsum('bchw,bciw->bhwi', q, k)
        diag = jnp.eye(h, dtype=bool)[:, None, :]
        energy_H = jnp.where(diag, -jnp.inf, energy_H)
        energy_W = jnp.einsum('bchw,bchj->bhwj', q, k)
        attn = jax.nn.softmax(jnp.concatenate([energy_H, energy_W], axis=-1), axis=-1)
        attn_H, attn_W = (attn[..., :h], attn[..., h:])
        out = jnp.einsum('bciw,bhwi->bchw', v, attn_H)
        out = out + jnp.einsum('bchj,bhwj->bchw', v, attn_W)
        return gamma[0] * out + x

    def _gn(v, G=32, eps=1e-5):
        B_, C_, H_, W_ = v.shape
        g = v.reshape(B_, G, C_ // G, H_, W_)
        m = jnp.mean(g, axis=(2, 3, 4), keepdims=True)
        s = jnp.var(g, axis=(2, 3, 4), keepdims=True)
        return ((g - m) / jnp.sqrt(s + eps)).reshape(v.shape)

    def _ln_c(v, eps=1e-6):
        m = jnp.mean(v, axis=1, keepdims=True)
        s = jnp.var(v, axis=1, keepdims=True)
        return (v - m) / jnp.sqrt(s + eps)

    def _ln_t(v, eps=1e-5):
        m = jnp.mean(v, axis=-1, keepdims=True)
        s = jnp.var(v, axis=-1, keepdims=True)
        return (v - m) / jnp.sqrt(s + eps)

    def _to_tokens(v):
        B_, C_, H_, W_ = v.shape
        return v.reshape(B_, C_, H_ * W_).transpose(0, 2, 1)
    def _from_tokens(t, like):
        B_, C_, H_, W_ = like.shape
        return t.transpose(0, 2, 1).reshape(B_, C_, H_, W_)

    x = _L0_conv_ref(x, L0_conv_Wq, L0_conv_bq, L0_conv_Wk, L0_conv_bk, L0_conv_Wv, L0_conv_bv, L0_conv_gamma)
    return x


_drawn_inputs = setup_inputs


def setup_inputs(seed=0):
    import zlib

    import numpy as np

    out = dict(_drawn_inputs(seed))
    spreads = {}
    factors = {}
    for name, (base, spread) in spreads.items():
        noise = np.random.default_rng([zlib.crc32(name.encode()), seed]).standard_normal(out[name].shape)
        drawn = base * np.exp(spread * noise) if base else spread * noise
        out[name] = jnp.asarray(drawn.astype(out[name].dtype))
    for name, factor in factors.items():
        out[name] = (out[name] * factor).astype(out[name].dtype)
    return out
```

```python
from contextlib import ExitStack

import concourse.bass as bass
from concourse import mybir

F32 = mybir.dt.float32
F32R = mybir.dt.float32r
BF16 = mybir.dt.bfloat16
ALU = mybir.AluOpType
ACT = mybir.ActivationFunctionType
AX_X = mybir.AxisListType.X

P = 128
B, C, H, W = 4, 512, 128, 128
CQ = C // 8
CK = C // P
LINES = 4
NG = H // LINES
TILE = LINES * C
GP = LINES * P
PAD = 1024
RROWS = 4
RCOLS = 2
MASK = -(2.0 ** 127)

CR_CHUNK = 4
CR_QK = 2
CR_ONE = 1
CR_Z = 8
CR_T = 2
CR_ZW = 2
CR_Y = 4
CR_ST = 16


def criss_cross(nc, x_rows, x_cols, w_qk, w_v, b_qk, b_v, gamma, scratch, out):
    ctx = ExitStack()
    with ctx:
        def sb(name, shape, dt=F32):
            return ctx.enter_context(nc.sbuf_tensor(name, shape, dt))

        def pb(name, shape, dt=F32):
            return ctx.enter_context(nc.psum_tensor(name, shape, dt))

        def sem(name):
            return ctx.enter_context(nc.semaphore(name))

        def f32(ap):
            return ap.bitcast(F32)

        def lines(ap):
            return ap.rearrange("p (r n) -> p r n", r=LINES)

        tiles = sb("tiles", [P, 4, TILE])
        x_hi = sb("x_hi", [P, CK, GP], F32R)
        x_lo = sb("x_lo", [P, CK, GP], F32R)
        qk = sb("qk", [P, H * W])
        q2 = sb("q2", [P, GP], F32R)
        k_hi2 = sb("k_hi2", [P, GP], F32R)
        k_lo0 = sb("k_lo0", [P, GP], F32R)
        shifted = sb("shifted", [P, GP])
        probs = sb("probs", [P, GP])
        pt_hi = sb("pt_hi", [P, 2, GP], F32R)
        pt_lo = sb("pt_lo", [P, 2, GP], F32R)
        t_hi = sb("t_hi", [P, 2, C], F32R)
        t_lo = sb("t_lo", [P, 2, C], F32R)
        xc_hi = sb("xc_hi", [P, 2, C], F32R)
        xc_lo = sb("xc_lo", [P, 2, C], F32R)
        xb = sb("xb", [P, CR_Y, C])
        joined = sb("joined", [P, 2, C])
        ost = sb("ost", [P, 2, TILE])
        wqk_hi = sb("wqk_hi", [P, CK, P], F32R)
        wqk_lo = sb("wqk_lo", [P, CK, P], F32R)
        wv_hi = sb("wv_hi", [P, CK, C], F32R)
        wv_lo = sb("wv_lo", [P, CK, C], F32R)
        gbv = sb("gbv", [P, C])
        bqk = sb("bqk", [P, 1])
        gam = sb("gam", [P, 1])
        ident = sb("ident", [P, P])
        ident_b = sb("ident_b", [P, P], BF16)
        mask_b = sb("mask_b", [P, GP], BF16)
        row_max = sb("row_max", [P, H])
        row_sum = sb("row_sum", [P, H])
        row_max_t = sb("row_max_t", [P, W])
        row_sum_t = sb("row_sum_t", [P, W])
        col_max = sb("col_max", [P, LINES])
        both_max = sb("both_max", [P, LINES])
        row_shift = sb("row_shift", [P, LINES])
        row_fac = sb("row_fac", [P, 2, LINES])
        sum_a = sb("sum_a", [P, LINES])
        sum_b = sb("sum_b", [P, LINES])
        sum_c = sb("sum_c", [P, LINES])
        sum_r = sb("sum_r", [P, LINES])
        scale = sb("scale", [P, 2, LINES])

        ps_y = [pb(f"ps_y{i}", [P, 512]) for i in range(2)]
        ps_t = [pb(f"ps_t{i}", [P, 512]) for i in range(2)]
        ps_z = [pb(f"ps_z{i}", [P, 512]) for i in range(2)]
        ps_e = pb("ps_e", [P, GP])
        ps_p = pb("ps_p", [P, GP])

        w_in = sem("w_in")
        x_in = [sem(f"x_in{i}") for i in range(4)]
        xc_in = [sem(f"xc_in{i}") for i in range(2)]
        zw_in = [sem(f"zw_in{i}") for i in range(2)]
        stored = [sem(f"stored{i}") for i in range(2)]
        ident_ok = sem("ident_ok")
        wsplit = sem("wsplit")
        xh_ok = sem("xh_ok")
        xh2_ok = sem("xh2_ok")
        xl_ok = sem("xl_ok")
        qk_mm = sem("qk_mm")
        qk_kept = sem("qk_kept")
        qk_split_hi = sem("qk_split_hi")
        qk_split = sem("qk_split")
        e_mm = sem("e_mm")
        max_ok = sem("max_ok")
        shift_ok = sem("shift_ok")
        exp_ok = sem("exp_ok")
        sum_ok = sem("sum_ok")
        p_mm = sem("p_mm")
        pth_ok = sem("pth_ok")
        ptl_ok = sem("ptl_ok")
        t_mm = sem("t_mm")
        th_ok = sem("th_ok")
        tl_ok = sem("tl_ok")
        z_mm = sem("z_mm")
        zw_ok = sem("zw_ok")
        stat_mm = sem("stat_mm")
        stat_ok = sem("stat_ok")
        small = sem("small")
        rfac_ok = sem("rfac_ok")
        xch_ok = sem("xch_ok")
        xcl_ok = sem("xcl_ok")
        xb_ok = sem("xb_ok")
        joined_ok = sem("joined_ok")
        y_mm = sem("y_mm")
        y_ok = sem("y_ok")
        SMALL = 6

        block = ctx.enter_context(nc.Block())

        class Group:

            def __init__(self, b, t, j, cols=False):
                ring = RCOLS if cols else RROWS
                self.b, self.cols = b, cols
                self.t, self.slot = t + j // ring, j % ring
                self.g = self.t * ring + self.slot
                self.n = b * NG + self.g
                self.q = b * (2 * NG) + self.g + cols * NG
                self.s = self.slot % 2
                self.pair = b * NG + (self.t + NG // 2 if cols else self.t * 2 + self.slot // 2)
                self.loads = b * (NG // ring) + self.t + 1

            def after(self, k):
                ring = RCOLS if self.cols else RROWS
                return Group(self.b, self.t, self.slot + k, self.cols) if self.slot + k < ring else \
                    Group(self.b, self.t + (self.slot + k) // ring, (self.slot + k) % ring, self.cols)

            def line(self, r):
                return self.n * LINES + r

            def all_line(self, r):
                return self.q * LINES + r

        def loop_groups(eng, b, cols, body):
            ring = RCOLS if cols else RROWS
            turns = NG // ring
            with eng.Fori(0, turns - 1) as t:
                for j in range(ring):
                    body(Group(b, t, j, cols), NG)
            for j in range(ring):
                body(Group(b, turns - 1, j, cols), ring - 1 - j)

        def loop_images(eng, rows, cols):
            with eng.Fori(0, B) as b:
                rows(b)
                cols(b)

        @block.sync
        def _(sp):
            sp.dma_start(ost[:, 0, :], w_v).then_inc(w_in, 16)
            sp.dma_start(ost[:, 1, 0:CK * P], w_qk).then_inc(w_in, 16)
            sp.dma_start(bqk[:, :], b_qk).then_inc(w_in, 16)
            sp.dma_start(gam[:, :], gamma.to_broadcast([P, 1])).then_inc(w_in, 16)
            sp.dma_start(gbv[:, :], b_v.to_broadcast([P, C])).then_inc(w_in, 16)
            for s in range(2):
                sp.sem_inc(stored[s], CR_ST)

            def load_rows(g):
                sp.dma_start(tiles[:, g.slot, :], x_rows[bass.ds(g.n, 1), :, :]
                             .rearrange("a p n -> p (a n)")).then_inc(x_in[g.slot], 16)

            def load_cols(g):
                sp.dma_start(tiles[:, g.s, :], x_cols[bass.ds(g.n, 1), :, :]
                             .rearrange("a p n -> p (a n)")).then_inc(xc_in[g.s], 16)

            def load_sums(g):
                sp.dma_start(tiles[:, 2 + g.s, :], scratch[bass.ds(g.b, 1), :, bass.ds(g.g * TILE, TILE)]
                             .rearrange("a p n -> p (a n)")).then_inc(zw_in[g.s], 16)

            def rows(b):
                for j in range(RROWS):
                    load_rows(Group(b, 0, j))

                def group(g, left):
                    if left >= RROWS:
                        sp.wait_ge(t_mm, g.all_line(LINES))
                        load_rows(g.after(RROWS))
                    sp.wait_ge(zw_ok, g.line(LINES) + CR_ZW)
                    sp.dma_start(scratch[bass.ds(b, 1), bass.ds(g.g * LINES, LINES), 0:W * C]
                                 .rearrange("a h (w c) -> w (a h) c", c=C),
                                 lines(ost[:, g.s, :])).then_inc(stored[g.s], 16)

                loop_groups(sp, b, False, group)

            def cols(b):
                load_cols(Group(b, 0, 0, True))
                for s in range(2):
                    sp.wait_ge(stored[s], (b * NG + NG // 2) * 16 + CR_ST)
                load_cols(Group(b, 0, 1, True))
                for s in range(2):
                    load_sums(Group(b, 0, s, True))

                def group(g, left):
                    if left >= RCOLS:
                        sp.wait_ge(xb_ok, g.line(LINES))
                        load_cols(g.after(RCOLS))
                        sp.wait_ge(joined_ok, g.line(LINES))
                        load_sums(g.after(RCOLS))
                    sp.wait_ge(y_ok, g.line(LINES) + CR_Y)
                    sp.dma_start(out[bass.ds(g.n, 1), :, :].rearrange("a p n -> p (a n)"),
                                 ost[:, g.s, :]).then_inc(stored[g.s], 16)

                loop_groups(sp, b, True, group)

            loop_images(sp, rows, cols)
            for s in range(2):
                sp.wait_ge(stored[s], B * NG * 16 + CR_ST)

        @block.gpsimd
        def _(pool):
            nc.gpsimd.memset(ident[:, :], 0.0).then_inc(ident_ok, 1)
            nc.gpsimd.memset(ident_b[:, :], 0.0).then_inc(ident_ok, 1)
            nc.gpsimd.memset(mask_b[:, :], 0.0).then_inc(ident_ok, 1)
            pool.wait_ge(ident_ok, 3)
            for m in (ident, ident_b):
                nc.gpsimd.affine_select(out=m[:, :], in_=m[:, :], compare_op=ALU.not_equal, fill=1.0,
                                        base=0, pattern=[[-1, P]], channel_multiplier=1).then_inc(ident_ok, 1)
            nc.gpsimd.affine_select(out=lines(mask_b[:, :]), in_=lines(mask_b[:, :]), compare_op=ALU.not_equal,
                                    fill=MASK, base=0, pattern=[[0, LINES], [-1, P]],
                                    channel_multiplier=1).then_inc(ident_ok, 1)
            pool.wait_ge(wsplit, 6)

            def rows(b):
                def group(g):
                    for ck in range(CK):
                        if ck == 2:
                            pool.wait_ge(xh2_ok, g.n + 1)
                        else:
                            pool.wait_ge(xh_ok, g.n * (CK - 1) + (3 if ck == 3 else ck + 1))
                        nc.gpsimd.tensor_tensor(x_lo[:, ck, :], tiles[:, g.slot, ck * GP:(ck + 1) * GP],
                                                f32(x_hi[:, ck, :]), ALU.subtract).then_inc(xl_ok, 1)

                with pool.Fori(0, NG // RROWS) as t:
                    for j in range(RROWS):
                        group(Group(b, t, j))

            def cols(b):
                def group(g):
                    for r in range(LINES):
                        x_line = tiles[:, g.s, r * C:(r + 1) * C]
                        pool.wait_ge(xch_ok, g.line(r + 1))
                        nc.gpsimd.tensor_tensor(xc_lo[:, r % 2, :], x_line, f32(xc_hi[:, r % 2, :]),
                                                ALU.subtract).then_inc(xcl_ok, 1)
                        pool.wait_ge(y_ok, g.line(r + 1) - CR_Y + CR_Y)
                        nc.gpsimd.tensor_tensor(xb[:, r, :], x_line, gbv[:, :], ALU.add).then_inc(xb_ok, 1)

                with pool.Fori(0, NG // RCOLS) as t:
                    for j in range(RCOLS):
                        group(Group(b, t, j, True))

            loop_images(pool, rows, cols)

        @block.scalar
        def _(act):
            act.sem_inc(qk_kept, CR_QK)
            act.sem_inc(exp_ok, CR_ONE)
            act.sem_inc(zw_ok, CR_ZW)
            act.wait_ge(w_in, 5 * 16)

            def x_high(g, ck):
                if ck == 2:
                    return
                if ck == 0:
                    act.wait_ge(x_in[g.slot], g.loads * 16)
                act.wait_ge(qk_mm, g.n * CK + ck + 1 - CR_CHUNK + CR_CHUNK)
                nc.scalar.activation(x_hi[:, ck, :], tiles[:, g.slot, ck * GP:(ck + 1) * GP],
                                     ACT.Copy).then_inc(xh_ok, 1)

            def keep_qk(g):
                act.wait_ge(qk_mm, (g.n + 1) * CK + CR_CHUNK)
                nc.scalar.activation(qk[:, bass.ds(g.g * GP, GP)], ps_y[g.s][:, :], ACT.Identity,
                                     bias=bqk[:, 0:1]).then_inc(qk_kept, 1)

            def t_high(g, r):
                act.wait_ge(t_mm, g.all_line(r + 1))
                nc.scalar.activation(t_hi[:, r % 2, :], ps_t[r % 2][:, :], ACT.Copy).then_inc(th_ok, 1)

            def exps(g):
                act.wait_ge(shift_ok, g.q + 1 + CR_ONE)
                act.wait_ge(p_mm, g.q + CR_ONE)
                nc.scalar.activation(probs[:, :], shifted[:, :], ACT.Exp).then_inc(exp_ok, 1)

            def pt_high(g):
                act.wait_ge(p_mm, g.q + 1 + CR_ONE)
                act.wait_ge(z_mm, g.all_line(0) - LINES + CR_Z)
                nc.scalar.activation(pt_hi[:, g.s, :], ps_p[:, :], ACT.Copy).then_inc(pth_ok, 1)

            def rows(b):
                def keep_sums(g, r):
                    if r == 0:
                        act.wait_ge(stored[g.s], g.pair * 16 + CR_ST)
                    act.wait_ge(z_mm, g.all_line(r + 1) + CR_Z)
                    nc.scalar.activation(ost[:, g.s, r * C:(r + 1) * C], ps_z[r % 2][:, :],
                                         ACT.Copy).then_inc(zw_ok, 1)

                g0, g1, g2 = (Group(b, 0, j) for j in range(3))
                for ck in range(CK):
                    x_high(g0, ck)
                x_high(g1, 0)
                x_high(g1, 1)
                keep_qk(g0)
                t_high(g0, 0)
                t_high(g0, 1)
                x_high(g1, 3)
                x_high(g2, 0)
                x_high(g2, 1)
                keep_qk(g1)
                exps(g0)
                pt_high(g0)
                x_high(g2, 3)

                def group(g, left):
                    for r in range(LINES):
                        if r == 2 and left >= 2:
                            keep_qk(g.after(2))
                        if r == 2 and left >= 1:
                            exps(g.after(1))
                        if r == 3 and left >= 1:
                            pt_high(g.after(1))
                        if left >= 3:
                            x_high(g.after(3), r)
                        keep_sums(g, r)
                        if r < 2:
                            t_high(g, r + 2)
                        elif left >= 1:
                            t_high(g.after(1), r - 2)

                loop_groups(act, b, False, group)

            def cols(b):
                def xc_high(g, r):
                    if r == 0:
                        act.wait_ge(xc_in[g.s], g.loads * 16)
                    act.wait_ge(z_mm, g.all_line(r) - 1 + CR_Z)
                    nc.scalar.activation(xc_hi[:, r % 2, :], tiles[:, g.s, r * C:(r + 1) * C],
                                         ACT.Copy).then_inc(xch_ok, 1)

                def row_factor(g):
                    act.wait_ge(small, g.n * SMALL + 2)
                    nc.scalar.activation(row_fac[:, g.s, :], row_shift[:, :], ACT.Exp).then_inc(rfac_ok, 1)

                g0 = Group(b, 0, 0, True)
                xc_high(g0, 0)
                xc_high(g0, 1)
                exps(g0)
                row_factor(g0)
                pt_high(g0)
                xc_high(g0, 2)
                t_high(g0, 0)

                def group(g, left):
                    for r in range(LINES):
                        if r == 0:
                            xc_high(g, 3)
                        elif left >= 1:
                            xc_high(g.after(1), r - 1)
                        if r < 3:
                            t_high(g, r + 1)
                        elif left >= 1:
                            t_high(g.after(1), 0)
                        if r == 0 and left >= 1:
                            exps(g.after(1))
                            row_factor(g.after(1))
                        if r == 1 and left >= 1:
                            pt_high(g.after(1))

                loop_groups(act, b, True, group)

            loop_images(act, rows, cols)

        @block.vector
        def _(dve):
            dve.sem_inc(shift_ok, CR_ONE)
            dve.sem_inc(ptl_ok, CR_ONE)
            dve.sem_inc(tl_ok, CR_T)
            dve.sem_inc(y_ok, CR_Y)
            dve.wait_ge(w_in, 5 * 16)
            w_v_in = ost[:, 0, :].rearrange("p (k n) -> p k n", k=CK)
            w_qk_in = ost[:, 1, 0:CK * P].rearrange("p (k n) -> p k n", k=CK)
            nc.vector.tensor_copy(wv_hi[:, :, :], w_v_in).then_inc(wsplit, 1)
            nc.vector.tensor_copy(wqk_hi[:, :, :], w_qk_in).then_inc(wsplit, 1)
            nc.vector.memset(f32(k_lo0[CQ:P, :]), 0.0).then_inc(wsplit, 1)
            nc.vector.tensor_scalar(gbv[:, :], gbv[:, :], gam[:, 0:1], None, ALU.mult).then_inc(wsplit, 1)
            dve.wait_ge(wsplit, 2)
            nc.vector.tensor_tensor(wv_lo[:, :, :], w_v_in, f32(wv_hi[:, :, :]), ALU.subtract).then_inc(wsplit, 1)
            nc.vector.tensor_tensor(wqk_lo[:, :, :], w_qk_in, f32(wqk_hi[:, :, :]), ALU.subtract).then_inc(wsplit, 1)

            def qk_lines(g):
                if g.cols:
                    v = qk[:, :].rearrange("p (h w) -> p w h", w=W)[:, bass.ds(g.g * LINES, LINES), :]
                else:
                    v = lines(qk[:, bass.ds(g.g * GP, GP)])
                return v[0:CQ], v[CQ:P]

            def split_high(g):
                if not g.cols:
                    dve.wait_ge(qk_kept, g.n + 1 + CR_QK)
                dve.wait_ge(e_mm, g.q + CR_ONE)
                q, k = qk_lines(g)
                nc.vector.tensor_copy(lines(q2[0:CQ, :]), q).then_inc(qk_split_hi, 1)
                nc.vector.tensor_copy(lines(k_hi2[CQ:P, :]), k).then_inc(qk_split_hi, 1)
                nc.vector.tensor_copy(lines(k_hi2[0:CQ, :]), k).then_inc(qk_split_hi, 1)

            def split_low(g):
                dve.wait_ge(qk_split_hi, 3 * g.q + 3)
                q, k = qk_lines(g)
                nc.vector.tensor_tensor(lines(q2[CQ:P, :]), q, lines(f32(q2[0:CQ, :])), ALU.subtract).then_inc(qk_split, 1)
                nc.vector.tensor_tensor(lines(k_lo0[0:CQ, :]), k, lines(f32(k_hi2[CQ:P, :])), ALU.subtract).then_inc(qk_split, 1)

            def spread(ap):
                return ap.unsqueeze(2).to_broadcast([P, LINES, P])

            def top_energy(g):
                dve.wait_ge(e_mm, g.q + 1 + CR_ONE)
                top = col_max[:, :] if g.cols else row_max[:, bass.ds(g.g * LINES, LINES)]
                nc.vector.reduce_max(top, lines(ps_e[:, :]), AX_X).then_inc(max_ok, 1)

            def joint_top(g):
                dve.wait_ge(max_ok, g.q + 1)
                nc.vector.tensor_tensor(both_max[:, :], col_max[:, :],
                                        row_max_t[:, bass.ds(g.g * LINES, LINES)], ALU.max).then_inc(small, 1)

            def shift(g):
                if g.cols:
                    dve.wait_ge(small, g.n * SMALL + 1)
                    top = both_max[:, :]
                else:
                    dve.wait_ge(max_ok, g.q + 1)
                    top = row_max[:, bass.ds(g.g * LINES, LINES)]
                dve.wait_ge(exp_ok, g.q + CR_ONE)
                nc.vector.tensor_tensor(lines(shifted[:, :]), lines(ps_e[:, :]), spread(top),
                                        ALU.subtract).then_inc(shift_ok, 1)

            def row_below(g):
                nc.vector.tensor_tensor(row_shift[:, :], row_max_t[:, bass.ds(g.g * LINES, LINES)],
                                        both_max[:, :], ALU.subtract).then_inc(small, 1)

            def total(g):
                dve.wait_ge(exp_ok, g.q + 1 + CR_ONE)
                sums = sum_a[:, :] if g.cols else row_sum[:, bass.ds(g.g * LINES, LINES)]
                nc.vector.reduce_sum(sums, lines(probs[:, :]), AX_X).then_inc(sum_ok, 1)

            def row_total(g):
                dve.wait_ge(rfac_ok, g.n + 1)
                nc.vector.tensor_tensor(sum_b[:, :], row_sum_t[:, bass.ds(g.g * LINES, LINES)],
                                        row_fac[:, g.s, :], ALU.mult).then_inc(small, 1)

            def both_totals(g):
                dve.wait_ge(sum_ok, g.q + 1)
                dve.wait_ge(small, g.n * SMALL + 3)
                nc.vector.tensor_tensor(sum_c[:, :], sum_a[:, :], sum_b[:, :], ALU.add).then_inc(small, 1)

            def inverse(g):
                dve.wait_ge(small, g.n * SMALL + 4)
                nc.vector.reciprocal(sum_r[:, :], sum_c[:, :]).then_inc(small, 1)

            def scales(g):
                dve.wait_ge(small, g.n * SMALL + 5)
                nc.vector.tensor_scalar(scale[:, g.s, :], sum_r[:, :], gam[:, 0:1], None, ALU.mult).then_inc(small, 1)

            def pt_low(g):
                dve.wait_ge(pth_ok, g.q + 1)
                nc.vector.tensor_tensor(pt_lo[:, g.s, :], ps_p[:, :], f32(pt_hi[:, g.s, :]),
                                        ALU.subtract).then_inc(ptl_ok, 1)

            def t_low(g, r):
                dve.wait_ge(th_ok, g.all_line(r + 1))
                nc.vector.tensor_tensor(t_lo[:, r % 2, :], ps_t[r % 2][:, :], f32(t_hi[:, r % 2, :]),
                                        ALU.subtract).then_inc(tl_ok, 1)

            def rows(b):
                def x_high(g):
                    dve.wait_ge(x_in[g.slot], g.loads * 16)
                    dve.wait_ge(qk_mm, g.n * CK + 3 - CR_CHUNK + CR_CHUNK)
                    nc.vector.tensor_copy(x_hi[:, 2, :], tiles[:, g.slot, 2 * GP:3 * GP]).then_inc(xh2_ok, 1)

                g0, g1, g2 = (Group(b, 0, j) for j in range(3))
                x_high(g0)
                x_high(g1)
                split_high(g0)
                split_low(g0)
                t_low(g0, 0)
                t_low(g0, 1)
                x_high(g2)
                top_energy(g0)
                shift(g0)
                split_high(g1)
                total(g0)
                pt_low(g0)
                split_low(g1)

                def group(g, left):
                    for r in range(LINES):
                        if r == 1 and left >= 1:
                            top_energy(g.after(1))
                            shift(g.after(1))
                        if r == 1 and left >= 3:
                            x_high(g.after(3))
                        if r == 3 and left >= 1:
                            pt_low(g.after(1))
                        if r == 2 and left >= 2:
                            split_high(g.after(2))
                        if r == 2 and left >= 1:
                            total(g.after(1))
                        if r < 2:
                            t_low(g, r + 2)
                        elif left >= 1:
                            t_low(g.after(1), r - 2)
                        if r == 3 and left >= 2:
                            split_low(g.after(2))

                loop_groups(dve, b, False, group)

            def cols(b):
                def join(g, r):
                    if r == 0:
                        dve.wait_ge(zw_in[g.s], g.loads * 16)
                    dve.wait_ge(z_mm, g.all_line(r + 1) + CR_Z)
                    nc.vector.scalar_tensor_tensor(out=joined[:, r % 2, :], in0=tiles[:, 2 + g.s, r * C:(r + 1) * C],
                                                   scalar=row_fac[:, g.s, r:r + 1], in1=ps_z[r % 2][:, :],
                                                   op0=ALU.mult, op1=ALU.add).then_inc(joined_ok, 1)

                def output(g, r):
                    if r == 0:
                        dve.wait_ge(stored[g.s], g.pair * 16 + CR_ST)
                        dve.wait_ge(small, g.n * SMALL + SMALL)
                    dve.wait_ge(xb_ok, g.line(r + 1))
                    dve.wait_ge(y_mm, g.line(r + 1))
                    nc.vector.scalar_tensor_tensor(out=ost[:, g.s, r * C:(r + 1) * C], in0=ps_y[r % 2][:, :],
                                                   scalar=scale[:, g.s, r:r + 1], in1=xb[:, r, :],
                                                   op0=ALU.mult, op1=ALU.add).then_inc(y_ok, 1)

                g0, g1 = Group(b, 0, 0, True), Group(b, 0, 1, True)
                split_high(g0)
                split_low(g0)
                dve.wait_ge(stat_mm, b + 1)
                nc.vector.tensor_copy(row_max_t[:, :], ps_y[0][:, 0:P]).then_inc(stat_ok, 1)
                nc.vector.tensor_copy(row_sum_t[:, :], ps_y[0][:, P:2 * P]).then_inc(stat_ok, 1)
                dve.wait_ge(stat_ok, 2 * b + 2)
                top_energy(g0)
                joint_top(g0)
                shift(g0)
                row_below(g0)
                split_high(g1)
                pt_low(g0)
                total(g0)
                row_total(g0)
                join(g0, 0)
                both_totals(g0)
                join(g0, 1)
                inverse(g0)
                t_low(g0, 0)
                scales(g0)
                split_low(g1)

                def group(g, left):
                    for r in range(LINES):
                        last = left < 1
                        if r == 0 and not last:
                            top_energy(g.after(1))
                        if r < 2:
                            join(g, r + 2)
                        elif not last:
                            join(g.after(1), r - 2)
                        if r == 0 and not last:
                            joint_top(g.after(1))
                        if r == 2 and not last:
                            both_totals(g.after(1))
                        if r == 3 and not last:
                            scales(g.after(1))
                        if r == 0 and not last:
                            shift(g.after(1))
                        if r < 3:
                            t_low(g, r + 1)
                        elif not last:
                            t_low(g.after(1), 0)
                        if r == 0 and not last:
                            row_below(g.after(1))
                        if r == 1 and not last:
                            pt_low(g.after(1))
                            total(g.after(1))
                            row_total(g.after(1))
                        if r == 2 and not last:
                            inverse(g.after(1))
                        if r == 2 and left >= 2:
                            split_high(g.after(2))
                        if r == 3 and left >= 2:
                            split_low(g.after(2))
                        output(g, r)

                loop_groups(dve, b, True, group)

            loop_images(dve, rows, cols)

        @block.tensor
        def _(pe):
            pe.sem_inc(qk_mm, CR_CHUNK)
            pe.sem_inc(e_mm, CR_ONE)
            pe.sem_inc(p_mm, CR_ONE)
            pe.sem_inc(z_mm, CR_Z)
            pe.wait_ge(ident_ok, 6)
            pe.wait_ge(wsplit, 6)

            def energies(g):
                pe.wait_ge(qk_split, 2 * g.q + 2)
                pe.wait_ge(shift_ok, g.q + CR_ONE)
                if g.cols:
                    nc.tensor.matmul(ps_e[:, :], ident_b[:, :], mask_b[:, :], start=True, stop=False)
                for r in range(LINES):
                    l = slice(r * P, (r + 1) * P)
                    nc.tensor.matmul(ps_e[:, l], q2[:, l], k_hi2[:, l], start=not g.cols, stop=False)
                    last = nc.tensor.matmul(ps_e[:, l], q2[:, l], k_lo0[:, l], start=False,
                                            stop=not g.cols or r == LINES - 1)
                last.then_inc(e_mm, 1)

            def transpose_probs(g):
                pe.wait_ge(exp_ok, g.q + 1 + CR_ONE)
                pe.wait_ge(ptl_ok, g.q + CR_ONE)
                for r in range(LINES):
                    l = slice(r * P, (r + 1) * P)
                    last = nc.tensor.transpose(ps_p[:, l], probs[:, l], ident[:, :])
                last.then_inc(p_mm, 1)

            def transpose_line(g, r, src):
                pe.wait_ge(tl_ok, g.all_line(r) - 1 + CR_T)
                for ck in range(CK):
                    last = nc.tensor.transpose(ps_t[r % 2][:, ck * P:(ck + 1) * P], src(ck), ident[:, :])
                last.then_inc(t_mm, 1)

            def sums(g, r, hi, lo):
                if r == 0:
                    pe.wait_ge(ptl_ok, g.q + 1 + CR_ONE)
                l = slice(r * P, (r + 1) * P)
                bank, s = ps_z[r % 2][:, :], r % 2
                nc.tensor.matmul(bank, pt_hi[:, g.s, l], hi[:, s, :], start=True, stop=False)
                nc.tensor.matmul(bank, pt_lo[:, g.s, l], hi[:, s, :], start=False, stop=False)
                nc.tensor.matmul(bank, pt_hi[:, g.s, l], lo[:, s, :], start=False, stop=True).then_inc(z_mm, 1)

            def rows(b):
                def project_qk(g, ck):
                    if ck == 0:
                        pe.wait_ge(qk_kept, g.n - 1 + CR_QK)
                    pe.wait_ge(xl_ok, g.n * CK + ck + 1)
                    bank = ps_y[g.s][:, :]
                    nc.tensor.matmul(bank, wqk_hi[:, ck, :], x_hi[:, ck, :], start=ck == 0, stop=False)
                    nc.tensor.matmul(bank, wqk_lo[:, ck, :], x_hi[:, ck, :], start=False, stop=False)
                    nc.tensor.matmul(bank, wqk_hi[:, ck, :], x_lo[:, ck, :], start=False,
                                     stop=ck == CK - 1).then_inc(qk_mm, 1)

                def transpose_x(g, r):
                    transpose_line(g, r, lambda ck: tiles[:, g.slot, ck * GP + r * P:ck * GP + (r + 1) * P])

                def row_sums(g, r):
                    pe.wait_ge(tl_ok, g.all_line(r + 1) + CR_T)
                    pe.wait_ge(zw_ok, g.line(r) - 1 + CR_ZW)
                    sums(g, r, t_hi, t_lo)

                g0, g1, g2 = (Group(b, 0, j) for j in range(3))
                pe.wait_ge(y_ok, b * W + CR_Y)
                for ck in range(CK):
                    project_qk(g0, ck)
                transpose_x(g0, 0)
                transpose_x(g0, 1)
                for ck in range(CK):
                    project_qk(g1, ck)
                energies(g0)
                project_qk(g2, 0)
                project_qk(g2, 1)
                transpose_probs(g0)

                def group(g, left):
                    for r in range(LINES):
                        if r == 1 and left >= 1:
                            energies(g.after(1))
                        row_sums(g, r)
                        if r < 2:
                            transpose_x(g, r + 2)
                        elif left >= 1:
                            transpose_x(g.after(1), r - 2)
                        if r < 2 and left >= 2:
                            project_qk(g.after(2), r + 2)
                        elif r >= 2 and left >= 3:
                            project_qk(g.after(3), r - 2)
                        if r == 2 and left >= 1:
                            transpose_probs(g.after(1))

                loop_groups(pe, b, False, group)

            def cols(b):
                def column_sums(g, r, first=False):
                    pe.wait_ge(xcl_ok, g.line(r + 1))
                    if first:
                        pe.wait_ge(zw_ok, (b + 1) * H + CR_ZW)
                    else:
                        pe.wait_ge(joined_ok, g.line(r) - 1)
                    sums(g, r, xc_hi, xc_lo)

                def transpose_joined(g, r):
                    pe.wait_ge(joined_ok, g.line(r + 1))
                    transpose_line(g, r, lambda ck: joined[:, r % 2, ck * P:(ck + 1) * P])

                def project_v(g, r):
                    pe.wait_ge(tl_ok, g.all_line(r + 1) + CR_T)
                    pe.wait_ge(y_ok, g.line(r) - 1 + CR_Y)
                    bank, s = ps_y[r % 2][:, :], r % 2
                    for ck in range(CK):
                        l = slice(ck * P, (ck + 1) * P)
                        nc.tensor.matmul(bank, t_hi[:, s, l], wv_hi[:, ck, :], start=ck == 0, stop=False)
                        nc.tensor.matmul(bank, t_hi[:, s, l], wv_lo[:, ck, :], start=False, stop=False)
                        last = nc.tensor.matmul(bank, t_lo[:, s, l], wv_hi[:, ck, :], start=False, stop=ck == CK - 1)
                    last.then_inc(y_mm, 1)

                g0 = Group(b, 0, 0, True)
                energies(g0)
                pe.wait_ge(sum_ok, b * 2 * NG + NG)
                nc.tensor.transpose(ps_y[0][:, 0:P], row_max[:, :], ident[:, :])
                nc.tensor.transpose(ps_y[0][:, P:2 * P], row_sum[:, :], ident[:, :]).then_inc(stat_mm, 1)
                transpose_probs(g0)
                column_sums(g0, 0, True)
                column_sums(g0, 1, True)
                transpose_joined(g0, 0)

                def group(g, left):
                    for r in range(LINES):
                        if r == 0 and left >= 1:
                            energies(g.after(1))
                        if r < 2:
                            column_sums(g, r + 2)
                        elif left >= 1:
                            column_sums(g.after(1), r - 2)
                        if r < 3:
                            transpose_joined(g, r + 1)
                        elif left >= 1:
                            transpose_joined(g.after(1), 0)
                        if r == 1 and left >= 1:
                            transpose_probs(g.after(1))
                        project_v(g, r)

                loop_groups(pe, b, True, group)

            loop_images(pe, rows, cols)


def kernel(**inputs):
    import concourse.bacc as bacc
    import numpy as np
    from concourse.bass_utils import run_bass_kernel_spmd

    x = np.asarray(inputs["x"])
    wq, wk, wv = (np.asarray(inputs[f"L0_conv_W{n}"]) for n in "qkv")
    bq, bk, bv = (np.asarray(inputs[f"L0_conv_b{n}"]) for n in "qkv")
    arrays = {
        "x_rows": x.reshape(B, CK, P, NG, GP).transpose(0, 3, 2, 1, 4).reshape(B * NG, P, TILE),
        "x_cols": x.reshape(B, C, H, NG, LINES).transpose(0, 3, 2, 4, 1).reshape(B * NG, P, TILE),
        "w_qk": np.concatenate([wq, wk]).reshape(P, CK, P).transpose(2, 1, 0).reshape(P, CK * P),
        "w_v": wv.reshape(C, CK, P).transpose(2, 1, 0).reshape(P, CK * C),
        "b_qk": np.concatenate([bq, bk]).reshape(P, 1),
        "b_v": bv.reshape(1, C),
        "gamma": np.asarray(inputs["L0_conv_gamma"]).reshape(1, 1),
    }
    arrays = {n: np.ascontiguousarray(a) for n, a in arrays.items()}
    nc = bacc.Bacc("TRN2", target_bir_lowering=False, num_devices=1)
    args = [nc.dram_tensor(n, a.shape, F32, kind="ExternalInput").ap() for n, a in arrays.items()]
    scratch = nc.dram_tensor("row_sums", (B, H, W * C + PAD), F32, kind="Internal").ap()
    out = nc.dram_tensor("out", (B * NG, P, TILE), F32, kind="ExternalOutput").ap()
    criss_cross(nc, *args, scratch, out)
    y = run_bass_kernel_spmd(nc, [arrays], core_ids=[0]).results[0]["out"]
    return np.ascontiguousarray(y.reshape(B, NG, H, LINES, C).transpose(0, 4, 2, 1, 3).reshape(B, C, H, W))
```

```python
from contextlib import ExitStack

import concourse.bass as bass
from concourse import mybir

F32 = mybir.dt.float32
F32R = mybir.dt.float32r
BF16 = mybir.dt.bfloat16
ALU = mybir.AluOpType
ACT = mybir.ActivationFunctionType
AX_X = mybir.AxisListType.X

P = 128
B, C, H, W = 4, 512, 128, 128
CQ = C // 8
CK = C // P
LINES = 4
NG = H // LINES
TILE = LINES * C
GP = LINES * P
PAD = 1024
RROWS = 4
RCOLS = 2
MASK = -(2.0 ** 127)

CR_CHUNK = 4
CR_QK = 2
CR_ONE = 1
CR_Z = 8
CR_T = 2
CR_ZW = 2
CR_Y = 4
CR_ST = 16


def criss_cross(nc, x_rows, x_cols, w_qk, w_v, b_qk, b_v, gamma, scratch, out):
    ctx = ExitStack()
    with ctx:
        def sb(name, shape, dt=F32):
            return ctx.enter_context(nc.sbuf_tensor(name, shape, dt))

        def pb(name, shape, dt=F32):
            return ctx.enter_context(nc.psum_tensor(name, shape, dt))

        def sem(name):
            return ctx.enter_context(nc.semaphore(name))

        def f32(ap):
            return ap.bitcast(F32)

        def lines(ap):
            return ap.rearrange("p (r n) -> p r n", r=LINES)

        tiles = sb("tiles", [P, 4, TILE])
        x_hi = sb("x_hi", [P, CK, GP], F32R)
        x_lo = sb("x_lo", [P, CK, GP], F32R)
        qk = sb("qk", [P, H * W])
        q2 = sb("q2", [P, GP], F32R)
        k_hi2 = sb("k_hi2", [P, GP], F32R)
        k_lo0 = sb("k_lo0", [P, GP], F32R)
        shifted = sb("shifted", [P, GP])
        probs = sb("probs", [P, GP])
        pt_hi = sb("pt_hi", [P, 2, GP], F32R)
        pt_lo = sb("pt_lo", [P, 2, GP], F32R)
        t_hi = sb("t_hi", [P, 2, C], F32R)
        t_lo = sb("t_lo", [P, 2, C], F32R)
        xc_hi = sb("xc_hi", [P, 2, C], F32R)
        xc_lo = sb("xc_lo", [P, 2, C], F32R)
        xb = sb("xb", [P, CR_Y, C])
        joined = sb("joined", [P, 2, C])
        ost = sb("ost", [P, 2, TILE])
        wqk_hi = sb("wqk_hi", [P, CK, P], F32R)
        wqk_lo = sb("wqk_lo", [P, CK, P], F32R)
        wv_hi = sb("wv_hi", [P, CK, C], F32R)
        wv_lo = sb("wv_lo", [P, CK, C], F32R)
        gbv = sb("gbv", [P, C])
        bqk = sb("bqk", [P, 1])
        gam = sb("gam", [P, 1])
        ident = sb("ident", [P, P])
        ident_b = sb("ident_b", [P, P], BF16)
        mask_b = sb("mask_b", [P, GP], BF16)
        row_max = sb("row_max", [P, H])
        row_sum = sb("row_sum", [P, H])
        row_max_t = sb("row_max_t", [P, W])
        row_sum_t = sb("row_sum_t", [P, W])
        col_max = sb("col_max", [P, LINES])
        both_max = sb("both_max", [P, LINES])
        row_shift = sb("row_shift", [P, LINES])
        row_fac = sb("row_fac", [P, 2, LINES])
        sum_a = sb("sum_a", [P, LINES])
        sum_b = sb("sum_b", [P, LINES])
        sum_c = sb("sum_c", [P, LINES])
        sum_r = sb("sum_r", [P, LINES])
        scale = sb("scale", [P, 2, LINES])

        ps_y = [pb(f"ps_y{i}", [P, 512]) for i in range(2)]
        ps_t = [pb(f"ps_t{i}", [P, 512]) for i in range(2)]
        ps_z = [pb(f"ps_z{i}", [P, 512]) for i in range(2)]
        ps_e = pb("ps_e", [P, GP])
        ps_p = pb("ps_p", [P, GP])

        w_in = sem("w_in")
        x_in = [sem(f"x_in{i}") for i in range(4)]
        xc_in = [sem(f"xc_in{i}") for i in range(2)]
        zw_in = [sem(f"zw_in{i}") for i in range(2)]
        zw0_in = sem("zw0_in")
        tail_stored = sem("tail_stored")
        stored = [sem(f"stored{i}") for i in range(2)]
        ident_ok = sem("ident_ok")
        wsplit = sem("wsplit")
        xh_ok = sem("xh_ok")
        xh2_ok = sem("xh2_ok")
        xl_ok = sem("xl_ok")
        qk_mm = sem("qk_mm")
        qk_kept = sem("qk_kept")
        qk_split_hi = sem("qk_split_hi")
        qk_split = sem("qk_split")
        e_mm = sem("e_mm")
        max_ok = sem("max_ok")
        shift_ok = sem("shift_ok")
        exp_ok = sem("exp_ok")
        sum_ok = sem("sum_ok")
        p_mm = sem("p_mm")
        pth_ok = sem("pth_ok")
        ptl_ok = sem("ptl_ok")
        t_mm = sem("t_mm")
        th_ok = sem("th_ok")
        tl_ok = sem("tl_ok")
        z_mm = sem("z_mm")
        zw_ok = sem("zw_ok")
        stat_mm = sem("stat_mm")
        stat_ok = sem("stat_ok")
        small = sem("small")
        rfac_ok = sem("rfac_ok")
        xch_ok = sem("xch_ok")
        xcl_ok = sem("xcl_ok")
        xb_ok = sem("xb_ok")
        joined_ok = sem("joined_ok")
        y_mm = sem("y_mm")
        y_ok = sem("y_ok")
        SMALL = 6

        block = ctx.enter_context(nc.Block())

        class Group:

            def __init__(self, b, t, j, cols=False):
                ring = RCOLS if cols else RROWS
                self.b, self.cols = b, cols
                self.t, self.slot = t + j // ring, j % ring
                self.g = self.t * ring + self.slot
                self.n = b * NG + self.g
                self.q = b * (2 * NG) + self.g + cols * NG
                self.s = self.slot % 2
                self.pair = b * NG + (self.t + NG // 2 if cols else self.t * 2 + self.slot // 2)
                self.loads = b * (NG // ring) + self.t + 1

            def after(self, k):
                ring = RCOLS if self.cols else RROWS
                return Group(self.b, self.t, self.slot + k, self.cols) if self.slot + k < ring else \
                    Group(self.b, self.t + (self.slot + k) // ring, (self.slot + k) % ring, self.cols)

            def line(self, r):
                return self.n * LINES + r

            def all_line(self, r):
                return self.q * LINES + r

        def loop_groups(eng, b, cols, body):
            ring = RCOLS if cols else RROWS
            turns = NG // ring
            with eng.Fori(0, turns - 1) as t:
                for j in range(ring):
                    body(Group(b, t, j, cols), NG)
            for j in range(ring):
                body(Group(b, turns - 1, j, cols), ring - 1 - j)

        def follows(g, left, k):
            return g.after(k) if left >= k else Group(g.b, 0, k - left - 1, True)

        def loop_images(eng, rows, cols):
            with eng.Fori(0, B - 1) as b:
                rows(b)
                cols(b, True)
            rows(B - 1)
            cols(B - 1, False)

        @block.sync
        def _(sp):
            sp.dma_start(ost[:, 0, :], w_v).then_inc(w_in, 16)
            sp.dma_start(ost[:, 1, 0:CK * P], w_qk).then_inc(w_in, 16)
            sp.dma_start(bqk[:, :], b_qk).then_inc(w_in, 16)
            sp.dma_start(gam[:, :], gamma.to_broadcast([P, 1])).then_inc(w_in, 16)
            sp.dma_start(gbv[:, :], b_v.to_broadcast([P, C])).then_inc(w_in, 16)
            for s in range(2):
                sp.sem_inc(stored[s], CR_ST)

            def load_rows(g):
                sp.dma_start(tiles[:, g.slot, :], x_rows[bass.ds(g.n, 1), :, :]
                             .rearrange("a p n -> p (a n)")).then_inc(x_in[g.slot], 16)

            def load_cols(g):
                sp.dma_start(tiles[:, 2 * g.s, :], x_cols[bass.ds(g.n, 1), :, :]
                             .rearrange("a p n -> p (a n)")).then_inc(xc_in[g.s], 16)

            def load_sums(g, first, past, arrived):
                sp.dma_start(tiles[:, 2 * g.s + 1, first * C:past * C],
                             scratch[bass.ds(g.b, 1), :, bass.ds(PAD + g.g * TILE + first * C, (past - first) * C)]
                             .rearrange("a p n -> p (a n)")).then_inc(arrived, 16)

            def store_sums(g, first, past, landed):
                sp.wait_ge(zw_ok, g.line(past) + CR_ZW)
                sp.dma_start(scratch[bass.ds(g.b, 1), bass.ds(g.g * LINES + first, past - first), PAD:PAD + W * C]
                             .rearrange("a h (w c) -> w (a h) c", c=C),
                             lines(ost[:, g.s, :])[:, first:past, :]).then_inc(landed, 16)

            def rows(b):
                def group(g, left):
                    if left >= RROWS:
                        sp.wait_ge(t_mm, g.all_line(LINES))
                        load_rows(g.after(RROWS))
                    elif g.s == 0:
                        sp.wait_ge(t_mm, g.all_line(LINES))
                        load_cols(Group(b, 0, g.slot // 2, True))
                    if left > 0:
                        store_sums(g, 0, LINES, stored[g.s])
                    else:
                        store_sums(g, 0, LINES - 1, tail_stored)
                        store_sums(g, LINES - 1, LINES, stored[g.s])

                loop_groups(sp, b, False, group)

            def cols(b, more):
                sp.wait_ge(stored[0], (b * NG + NG // 2) * 16 + CR_ST)
                sp.wait_ge(stored[1], (b * NG + NG // 2) * 16 + CR_ST)
                sp.wait_ge(tail_stored, b * 16 + 16)
                load_sums(Group(b, 0, 0, True), 0, 1, zw0_in)
                load_sums(Group(b, 0, 0, True), 1, LINES, zw_in[0])
                load_sums(Group(b, 0, 1, True), 0, LINES, zw_in[1])

                def group(g, left):
                    if left >= RCOLS or more:
                        sp.wait_ge(xb_ok, g.line(LINES))
                        if left >= RCOLS:
                            load_cols(g.after(RCOLS))
                        else:
                            load_rows(Group(b + 1, 0, 2 * g.s))
                        sp.wait_ge(joined_ok, g.line(LINES))
                        if left >= RCOLS:
                            load_sums(g.after(RCOLS), 0, LINES, zw_in[g.s])
                        else:
                            load_rows(Group(b + 1, 0, 2 * g.s + 1))
                    sp.wait_ge(y_ok, g.line(LINES) + CR_Y)
                    sp.dma_start(out[bass.ds(g.n, 1), :, :].rearrange("a p n -> p (a n)"),
                                 ost[:, g.s, :]).then_inc(stored[g.s], 16)

                loop_groups(sp, b, True, group)

            for j in range(RROWS):
                load_rows(Group(0, 0, j))
            loop_images(sp, rows, cols)
            for s in range(2):
                sp.wait_ge(stored[s], B * NG * 16 + CR_ST)

        @block.gpsimd
        def _(pool):
            nc.gpsimd.memset(ident[:, :], 0.0).then_inc(ident_ok, 1)
            nc.gpsimd.memset(ident_b[:, :], 0.0).then_inc(ident_ok, 1)
            nc.gpsimd.memset(mask_b[:, :], 0.0).then_inc(ident_ok, 1)
            pool.wait_ge(ident_ok, 3)
            for m in (ident, ident_b):
                nc.gpsimd.affine_select(out=m[:, :], in_=m[:, :], compare_op=ALU.not_equal, fill=1.0,
                                        base=0, pattern=[[-1, P]], channel_multiplier=1).then_inc(ident_ok, 1)
            nc.gpsimd.affine_select(out=lines(mask_b[:, :]), in_=lines(mask_b[:, :]), compare_op=ALU.not_equal,
                                    fill=MASK, base=0, pattern=[[0, LINES], [-1, P]],
                                    channel_multiplier=1).then_inc(ident_ok, 1)
            pool.wait_ge(wsplit, 6)

            def x_low(g, ck):
                if ck == 2:
                    pool.wait_ge(xh2_ok, g.n + 1)
                else:
                    pool.wait_ge(xh_ok, g.n * (CK - 1) + (3 if ck == 3 else ck + 1))
                nc.gpsimd.tensor_tensor(x_lo[:, ck, :], tiles[:, g.slot, ck * GP:(ck + 1) * GP],
                                        f32(x_hi[:, ck, :]), ALU.subtract).then_inc(xl_ok, 1)

            def rows(b):
                def group(g, left):
                    if left >= 1:
                        for ck in range(CK):
                            x_low(g.after(1), ck)

                loop_groups(pool, b, False, group)

            def cols(b, more):
                def group(g, left):
                    for r in range(LINES):
                        x_line = tiles[:, 2 * g.s, r * C:(r + 1) * C]
                        pool.wait_ge(xch_ok, g.line(r + 1))
                        nc.gpsimd.tensor_tensor(xc_lo[:, r % 2, :], x_line, f32(xc_hi[:, r % 2, :]),
                                                ALU.subtract).then_inc(xcl_ok, 1)
                        pool.wait_ge(y_ok, g.line(r + 1) - CR_Y + CR_Y)
                        nc.gpsimd.tensor_tensor(xb[:, r, :], x_line, gbv[:, :], ALU.add).then_inc(xb_ok, 1)
                    if left == 0 and more:
                        for ck in range(CK):
                            x_low(Group(b + 1, 0, 0), ck)

                loop_groups(pool, b, True, group)

            for ck in range(CK):
                x_low(Group(0, 0, 0), ck)
            loop_images(pool, rows, cols)

        @block.scalar
        def _(act):
            act.sem_inc(qk_kept, CR_QK)
            act.sem_inc(exp_ok, CR_ONE)
            act.sem_inc(zw_ok, CR_ZW)
            act.wait_ge(w_in, 5 * 16)

            def x_high(g, ck):
                if ck == 2:
                    return
                if ck == 0:
                    act.wait_ge(x_in[g.slot], g.loads * 16)
                act.wait_ge(qk_mm, g.n * CK + ck + 1 - CR_CHUNK + CR_CHUNK)
                nc.scalar.activation(x_hi[:, ck, :], tiles[:, g.slot, ck * GP:(ck + 1) * GP],
                                     ACT.Copy).then_inc(xh_ok, 1)

            def keep_qk(g, first=False):
                act.wait_ge(qk_mm, (g.n + 1) * CK + CR_CHUNK)
                nc.scalar.activation(qk[:, bass.ds(g.g * GP, GP)], (ps_p if first else ps_y[1 - g.s])[:, :], ACT.Identity,
                                     bias=bqk[:, 0:1]).then_inc(qk_kept, 1)

            def t_high(g, r):
                act.wait_ge(t_mm, g.all_line(r + 1))
                nc.scalar.activation(t_hi[:, r % 2, :], ps_t[r % 2][:, :], ACT.Copy).then_inc(th_ok, 1)

            def exps(g):
                act.wait_ge(shift_ok, g.q + 1 + CR_ONE)
                act.wait_ge(p_mm, g.q + CR_ONE)
                nc.scalar.activation(probs[:, :], shifted[:, :], ACT.Exp).then_inc(exp_ok, 1)

            def pt_high(g):
                act.wait_ge(p_mm, g.q + 1 + CR_ONE)
                act.wait_ge(z_mm, g.all_line(0) - LINES + CR_Z)
                nc.scalar.activation(pt_hi[:, g.s, :], ps_p[:, :], ACT.Copy).then_inc(pth_ok, 1)

            def xc_high(g, r, first=False):
                if r == 0:
                    act.wait_ge(xc_in[g.s], g.loads * 16)
                if not first:
                    act.wait_ge(z_mm, g.all_line(r) - 1 + CR_Z)
                nc.scalar.activation(xc_hi[:, r % 2, :], tiles[:, 2 * g.s, r * C:(r + 1) * C],
                                     ACT.Copy).then_inc(xch_ok, 1)

            def row_factor(g):
                act.wait_ge(small, g.n * SMALL + 2)
                nc.scalar.activation(row_fac[:, g.s, :], row_shift[:, :], ACT.Exp).then_inc(rfac_ok, 1)

            def rows_lead(b, step):
                g0, g1, g2 = (Group(b, 0, j) for j in range(3))
                if step == 0:
                    x_high(g0, 0)
                if step == 1:
                    x_high(g0, 1)
                if step == 2:
                    x_high(g0, 3)
                if step == 4:
                    x_high(g1, 0)
                    x_high(g1, 1)
                    keep_qk(g0, True)
                if step == 5:
                    t_high(g0, 0)
                    x_high(g1, 3)
                    exps(g0)
                if step == 6:
                    t_high(g0, 1)
                    x_high(g2, 0)
                    pt_high(g0)
                    x_high(g2, 1)
                    keep_qk(g1)
                    x_high(g2, 3)

            def rows(b):
                def keep_sums(g, r):
                    if r == 0:
                        act.wait_ge(stored[g.s], g.pair * 16 + CR_ST)
                    act.wait_ge(z_mm, g.all_line(r + 1) + CR_Z)
                    nc.scalar.activation(ost[:, g.s, r * C:(r + 1) * C], ps_z[r % 2][:, :],
                                         ACT.Copy).then_inc(zw_ok, 1)

                def group(g, left):
                    for r in range(LINES):
                        if r != 2:
                            keep_sums(g, r)
                        if r == 1:
                            t_high(g, 3)
                            exps(follows(g, left, 1))
                            if left == 0:
                                row_factor(follows(g, left, 1))
                            if left >= 2:
                                keep_qk(g.after(2))
                        if r == 2:
                            pt_high(follows(g, left, 1))
                        if r == 0:
                            t_high(g, 2)
                        if r >= 2 and left >= 1:
                            t_high(g.after(1), r - 2)
                        if r == 2:
                            keep_sums(g, r)
                        if left >= 3:
                            x_high(g.after(3), r)
                        if r < 2 and left == 0:
                            xc_high(follows(g, left, 1), r, True)

                rows_lead(b, 6)
                loop_groups(act, b, False, group)

            def cols(b, more):
                g0 = Group(b, 0, 0, True)
                xc_high(g0, 2)
                t_high(g0, 0)

                def group(g, left):
                    for r in range(LINES):
                        if r == 0:
                            xc_high(g, 3)
                        elif left >= 1:
                            xc_high(g.after(1), r - 1)
                        if r < 3:
                            t_high(g, r + 1)
                        elif left >= 1:
                            t_high(g.after(1), 0)
                        if r == 0 and left >= 1:
                            exps(g.after(1))
                            row_factor(g.after(1))
                        if r == 1 and left >= 1:
                            pt_high(g.after(1))
                        if more and r >= 2 * left:
                            rows_lead(b + 1, r + 2 - left * LINES)

                loop_groups(act, b, True, group)

            for step in range(6):
                rows_lead(0, step)
            loop_images(act, rows, cols)

        @block.vector
        def _(dve):
            dve.sem_inc(shift_ok, CR_ONE)
            dve.sem_inc(ptl_ok, CR_ONE)
            dve.sem_inc(tl_ok, CR_T)
            dve.sem_inc(y_ok, CR_Y)
            dve.wait_ge(w_in, 5 * 16)
            w_v_in = ost[:, 0, :].rearrange("p (k n) -> p k n", k=CK)
            w_qk_in = ost[:, 1, 0:CK * P].rearrange("p (k n) -> p k n", k=CK)
            nc.vector.tensor_copy(wv_hi[:, :, :], w_v_in).then_inc(wsplit, 1)
            nc.vector.tensor_copy(wqk_hi[:, :, :], w_qk_in).then_inc(wsplit, 1)
            nc.vector.memset(f32(k_lo0[CQ:P, :]), 0.0).then_inc(wsplit, 1)
            nc.vector.tensor_scalar(gbv[:, :], gbv[:, :], gam[:, 0:1], None, ALU.mult).then_inc(wsplit, 1)
            dve.wait_ge(wsplit, 2)
            nc.vector.tensor_tensor(wv_lo[:, :, :], w_v_in, f32(wv_hi[:, :, :]), ALU.subtract).then_inc(wsplit, 1)
            nc.vector.tensor_tensor(wqk_lo[:, :, :], w_qk_in, f32(wqk_hi[:, :, :]), ALU.subtract).then_inc(wsplit, 1)

            def qk_lines(g):
                if g.cols:
                    v = qk[:, :].rearrange("p (h w) -> p w h", w=W)[:, bass.ds(g.g * LINES, LINES), :]
                else:
                    v = lines(qk[:, bass.ds(g.g * GP, GP)])
                return v[0:CQ], v[CQ:P]

            def split_high(g):
                if not g.cols:
                    dve.wait_ge(qk_kept, g.n + 1 + CR_QK)
                dve.wait_ge(e_mm, g.q + CR_ONE)
                q, k = qk_lines(g)
                nc.vector.tensor_copy(lines(q2[0:CQ, :]), q).then_inc(qk_split_hi, 1)
                nc.vector.tensor_copy(lines(k_hi2[CQ:P, :]), k).then_inc(qk_split_hi, 1)
                nc.vector.tensor_copy(lines(k_hi2[0:CQ, :]), k).then_inc(qk_split_hi, 1)

            def split_low(g):
                dve.wait_ge(qk_split_hi, 3 * g.q + 3)
                q, k = qk_lines(g)
                nc.vector.tensor_tensor(lines(q2[CQ:P, :]), q, lines(f32(q2[0:CQ, :])), ALU.subtract).then_inc(qk_split, 1)
                nc.vector.tensor_tensor(lines(k_lo0[0:CQ, :]), k, lines(f32(k_hi2[CQ:P, :])), ALU.subtract).then_inc(qk_split, 1)

            def spread(ap):
                return ap.unsqueeze(2).to_broadcast([P, LINES, P])

            def top_energy(g):
                dve.wait_ge(e_mm, g.q + 1 + CR_ONE)
                top = col_max[:, :] if g.cols else row_max[:, bass.ds(g.g * LINES, LINES)]
                nc.vector.reduce_max(top, lines(ps_e[:, :]), AX_X).then_inc(max_ok, 1)

            def joint_top(g):
                dve.wait_ge(max_ok, g.q + 1)
                nc.vector.tensor_tensor(both_max[:, :], col_max[:, :],
                                        row_max_t[:, bass.ds(g.g * LINES, LINES)], ALU.max).then_inc(small, 1)

            def shift(g):
                if g.cols:
                    dve.wait_ge(small, g.n * SMALL + 1)
                    top = both_max[:, :]
                else:
                    dve.wait_ge(max_ok, g.q + 1)
                    top = row_max[:, bass.ds(g.g * LINES, LINES)]
                dve.wait_ge(exp_ok, g.q + CR_ONE)
                nc.vector.tensor_tensor(lines(shifted[:, :]), lines(ps_e[:, :]), spread(top),
                                        ALU.subtract).then_inc(shift_ok, 1)

            def row_below(g):
                nc.vector.tensor_tensor(row_shift[:, :], row_max_t[:, bass.ds(g.g * LINES, LINES)],
                                        both_max[:, :], ALU.subtract).then_inc(small, 1)

            def total(g):
                dve.wait_ge(exp_ok, g.q + 1 + CR_ONE)
                sums = sum_a[:, :] if g.cols else row_sum[:, bass.ds(g.g * LINES, LINES)]
                nc.vector.reduce_sum(sums, lines(probs[:, :]), AX_X).then_inc(sum_ok, 1)

            def row_total(g):
                dve.wait_ge(rfac_ok, g.n + 1)
                nc.vector.tensor_tensor(sum_b[:, :], row_sum_t[:, bass.ds(g.g * LINES, LINES)],
                                        row_fac[:, g.s, :], ALU.mult).then_inc(small, 1)

            def both_totals(g):
                dve.wait_ge(sum_ok, g.q + 1)
                dve.wait_ge(small, g.n * SMALL + 3)
                nc.vector.tensor_tensor(sum_c[:, :], sum_a[:, :], sum_b[:, :], ALU.add).then_inc(small, 1)

            def inverse(g):
                dve.wait_ge(small, g.n * SMALL + 4)
                nc.vector.reciprocal(sum_r[:, :], sum_c[:, :]).then_inc(small, 1)

            def scales(g):
                dve.wait_ge(small, g.n * SMALL + 5)
                nc.vector.tensor_scalar(scale[:, g.s, :], sum_r[:, :], gam[:, 0:1], None, ALU.mult).then_inc(small, 1)

            def pt_low(g):
                dve.wait_ge(pth_ok, g.q + 1)
                nc.vector.tensor_tensor(pt_lo[:, g.s, :], ps_p[:, :], f32(pt_hi[:, g.s, :]),
                                        ALU.subtract).then_inc(ptl_ok, 1)

            def t_low(g, r):
                dve.wait_ge(th_ok, g.all_line(r + 1))
                nc.vector.tensor_tensor(t_lo[:, r % 2, :], ps_t[r % 2][:, :], f32(t_hi[:, r % 2, :]),
                                        ALU.subtract).then_inc(tl_ok, 1)

            def x_high(g):
                dve.wait_ge(x_in[g.slot], g.loads * 16)
                dve.wait_ge(qk_mm, g.n * CK + 3 - CR_CHUNK + CR_CHUNK)
                nc.vector.tensor_copy(x_hi[:, 2, :], tiles[:, g.slot, 2 * GP:3 * GP]).then_inc(xh2_ok, 1)

            def rows_lead(b, step):
                g0, g1, g2 = (Group(b, 0, j) for j in range(3))
                if step == 2:
                    x_high(g0)
                if step == 4:
                    split_high(g0)
                    split_low(g0)
                if step == 5:
                    x_high(g1)
                    t_low(g0, 0)
                    top_energy(g0)
                    shift(g0)
                if step == 6:
                    t_low(g0, 1)
                    total(g0)
                    pt_low(g0)
                    split_high(g1)
                    x_high(g2)
                    split_low(g1)

            def rows(b):
                def group(g, left):
                    for r in range(LINES):
                        if r == 1:
                            if left == 0:
                                dve.wait_ge(stat_mm, b + 1)
                                nc.vector.tensor_copy(row_max_t[:, :], ps_y[0][:, 0:P]).then_inc(stat_ok, 1)
                                nc.vector.tensor_copy(row_sum_t[:, :], ps_y[0][:, P:2 * P]).then_inc(stat_ok, 1)
                            top_energy(follows(g, left, 1))
                            if left == 0:
                                dve.wait_ge(stat_ok, 2 * b + 2)
                                joint_top(follows(g, left, 1))
                            shift(follows(g, left, 1))
                            if left == 0:
                                row_below(follows(g, left, 1))
                        if r == 1 and left >= 3:
                            x_high(g.after(3))
                        if r == 2:
                            split_high(follows(g, left, 2))
                            pt_low(follows(g, left, 1))
                        if r == 3:
                            split_low(follows(g, left, 2))
                        if r < 2:
                            t_low(g, r + 2)
                        elif left >= 1:
                            t_low(g.after(1), r - 2)
                        if r == 3:
                            total(follows(g, left, 1))

                rows_lead(b, 6)
                loop_groups(dve, b, False, group)

            def cols(b, more):
                def join(g, r, first=0):
                    if first and r == 0:
                        dve.wait_ge(zw0_in, b * 16 + 16)
                    elif r == first:
                        dve.wait_ge(zw_in[g.s], g.loads * 16)
                    dve.wait_ge(z_mm, g.all_line(r + 1) + CR_Z)
                    nc.vector.scalar_tensor_tensor(out=joined[:, r % 2, :], in0=tiles[:, 2 * g.s + 1, r * C:(r + 1) * C],
                                                   scalar=row_fac[:, g.s, r:r + 1], in1=ps_z[r % 2][:, :],
                                                   op0=ALU.mult, op1=ALU.add).then_inc(joined_ok, 1)

                def output(g, r):
                    if r == 0:
                        dve.wait_ge(stored[g.s], g.pair * 16 + CR_ST)
                        dve.wait_ge(small, g.n * SMALL + SMALL)
                    dve.wait_ge(xb_ok, g.line(r + 1))
                    dve.wait_ge(y_mm, g.line(r + 1))
                    nc.vector.scalar_tensor_tensor(out=ost[:, g.s, r * C:(r + 1) * C], in0=ps_y[r % 2][:, :],
                                                   scalar=scale[:, g.s, r:r + 1], in1=xb[:, r, :],
                                                   op0=ALU.mult, op1=ALU.add).then_inc(y_ok, 1)

                g0 = Group(b, 0, 0, True)
                row_total(g0)
                both_totals(g0)
                inverse(g0)
                scales(g0)
                join(g0, 0, 1)
                join(g0, 1, 1)
                t_low(g0, 0)

                def group(g, left):
                    for r in range(LINES):
                        last = left < 1
                        if r == 0 and not last:
                            top_energy(g.after(1))
                        if r < 2:
                            join(g, r + 2)
                        elif not last:
                            join(g.after(1), r - 2)
                        if r == 0 and not last:
                            joint_top(g.after(1))
                        if r == 2 and not last:
                            both_totals(g.after(1))
                        if r == 3 and not last:
                            scales(g.after(1))
                        if r == 3 and left >= 2:
                            split_low(g.after(2))
                        if r == 0 and not last:
                            shift(g.after(1))
                        if r < 3:
                            t_low(g, r + 1)
                        elif not last:
                            t_low(g.after(1), 0)
                        if r == 0 and not last:
                            row_below(g.after(1))
                        if r == 1 and not last:
                            pt_low(g.after(1))
                            total(g.after(1))
                            row_total(g.after(1))
                        if r == 2 and not last:
                            inverse(g.after(1))
                        if r == 2 and left >= 2:
                            split_high(g.after(2))
                        if more and r >= 2 * left:
                            rows_lead(b + 1, r + 2 - left * LINES)
                        output(g, r)

                loop_groups(dve, b, True, group)

            for step in range(6):
                rows_lead(0, step)
            loop_images(dve, rows, cols)

        @block.tensor
        def _(pe):
            pe.sem_inc(qk_mm, CR_CHUNK)
            pe.sem_inc(e_mm, CR_ONE)
            pe.sem_inc(p_mm, CR_ONE)
            pe.sem_inc(z_mm, CR_Z)
            pe.wait_ge(ident_ok, 6)
            pe.wait_ge(wsplit, 6)

            def energies(g):
                pe.wait_ge(qk_split, 2 * g.q + 2)
                pe.wait_ge(shift_ok, g.q + CR_ONE)
                if g.cols:
                    nc.tensor.matmul(ps_e[:, :], ident_b[:, :], mask_b[:, :], start=True, stop=False)
                for r in range(LINES):
                    l = slice(r * P, (r + 1) * P)
                    nc.tensor.matmul(ps_e[:, l], q2[:, l], k_hi2[:, l], start=not g.cols, stop=False)
                    last = nc.tensor.matmul(ps_e[:, l], q2[:, l], k_lo0[:, l], start=False,
                                            stop=not g.cols or r == LINES - 1)
                last.then_inc(e_mm, 1)

            def transpose_probs(g):
                pe.wait_ge(exp_ok, g.q + 1 + CR_ONE)
                pe.wait_ge(ptl_ok, g.q + CR_ONE)
                for r in range(LINES):
                    l = slice(r * P, (r + 1) * P)
                    last = nc.tensor.transpose(ps_p[:, l], probs[:, l], ident[:, :])
                last.then_inc(p_mm, 1)

            def transpose_line(g, r, src):
                pe.wait_ge(tl_ok, g.all_line(r) - 1 + CR_T)
                for ck in range(CK):
                    last = nc.tensor.transpose(ps_t[r % 2][:, ck * P:(ck + 1) * P], src(ck), ident[:, :])
                last.then_inc(t_mm, 1)

            def sums(g, r, hi, lo):
                if r == 0:
                    pe.wait_ge(ptl_ok, g.q + 1 + CR_ONE)
                l = slice(r * P, (r + 1) * P)
                bank, s = ps_z[r % 2][:, :], r % 2
                nc.tensor.matmul(bank, pt_hi[:, g.s, l], hi[:, s, :], start=True, stop=False)
                nc.tensor.matmul(bank, pt_lo[:, g.s, l], hi[:, s, :], start=False, stop=False)
                nc.tensor.matmul(bank, pt_hi[:, g.s, l], lo[:, s, :], start=False, stop=True).then_inc(z_mm, 1)

            def project_qk(g, ck, first=0):
                if ck == 0:
                    if first == 1:
                        pe.wait_ge(ptl_ok, g.q + CR_ONE)
                    elif first:
                        pe.wait_ge(y_ok, g.b * W - (first == 2) + CR_Y)
                    else:
                        pe.wait_ge(qk_kept, g.n - 1 + CR_QK)
                pe.wait_ge(xl_ok, g.n * CK + ck + 1)
                bank = (ps_p if first == 1 else ps_y[1 - g.s])[:, :]
                nc.tensor.matmul(bank, wqk_hi[:, ck, :], x_hi[:, ck, :], start=ck == 0, stop=False)
                nc.tensor.matmul(bank, wqk_lo[:, ck, :], x_hi[:, ck, :], start=False, stop=False)
                nc.tensor.matmul(bank, wqk_hi[:, ck, :], x_lo[:, ck, :], start=False,
                                 stop=ck == CK - 1).then_inc(qk_mm, 1)

            def transpose_x(g, r):
                transpose_line(g, r, lambda ck: tiles[:, g.slot, ck * GP + r * P:ck * GP + (r + 1) * P])

            def rows_lead(b, step):
                g0, g1, g2 = (Group(b, 0, j) for j in range(3))
                if step == 3:
                    project_qk(g0, 0, 1)
                    project_qk(g0, 1, 1)
                if step == 4:
                    project_qk(g0, 2, 1)
                    project_qk(g0, 3, 1)
                if step == 5:
                    transpose_x(g0, 0)
                    energies(g0)
                if step == 6:
                    transpose_x(g0, 1)
                    project_qk(g1, 0, 2)
                    project_qk(g1, 1, 2)
                    transpose_probs(g0)
                    project_qk(g1, 2, 2)
                    project_qk(g1, 3, 2)
                    project_qk(g2, 0, 3)
                    project_qk(g2, 1, 3)

            def rows(b):
                def row_sums(g, r):
                    pe.wait_ge(tl_ok, g.all_line(r + 1) + CR_T)
                    pe.wait_ge(zw_ok, g.line(r) - 1 + CR_ZW)
                    sums(g, r, t_hi, t_lo)

                def group(g, left):
                    for r in range(LINES):
                        if r == 1:
                            if left == 0:
                                pe.wait_ge(sum_ok, b * 2 * NG + NG)
                                nc.tensor.transpose(ps_y[0][:, 0:P], row_max[:, :], ident[:, :])
                                nc.tensor.transpose(ps_y[0][:, P:2 * P], row_sum[:, :], ident[:, :]).then_inc(stat_mm, 1)
                            energies(follows(g, left, 1))
                        row_sums(g, r)
                        if r < 2:
                            transpose_x(g, r + 2)
                        elif left >= 1:
                            transpose_x(g.after(1), r - 2)
                        if r == 2:
                            transpose_probs(follows(g, left, 1))
                        if r < 2 and left >= 2:
                            project_qk(g.after(2), r + 2)
                        elif r >= 2 and left >= 3:
                            project_qk(g.after(3), r - 2)
                rows_lead(b, 6)
                loop_groups(pe, b, False, group)

            def cols(b, more):
                def column_sums(g, r, first=False):
                    pe.wait_ge(xcl_ok, g.line(r + 1))
                    if first:
                        pe.wait_ge(zw_ok, b * H + H - 1 + r + CR_ZW)
                    else:
                        pe.wait_ge(joined_ok, g.line(r) - 1)
                    sums(g, r, xc_hi, xc_lo)

                def transpose_joined(g, r):
                    pe.wait_ge(joined_ok, g.line(r + 1))
                    transpose_line(g, r, lambda ck: joined[:, r % 2, ck * P:(ck + 1) * P])

                def project_v(g, r):
                    pe.wait_ge(tl_ok, g.all_line(r + 1) + CR_T)
                    pe.wait_ge(y_ok, g.line(r) - 1 + CR_Y)
                    bank, s = ps_y[r % 2][:, :], r % 2
                    for ck in range(CK):
                        l = slice(ck * P, (ck + 1) * P)
                        nc.tensor.matmul(bank, t_hi[:, s, l], wv_hi[:, ck, :], start=ck == 0, stop=False)
                        nc.tensor.matmul(bank, t_hi[:, s, l], wv_lo[:, ck, :], start=False, stop=False)
                        last = nc.tensor.matmul(bank, t_lo[:, s, l], wv_hi[:, ck, :], start=False, stop=ck == CK - 1)
                    last.then_inc(y_mm, 1)

                g0 = Group(b, 0, 0, True)
                column_sums(g0, 0, True)
                column_sums(g0, 1, True)
                transpose_joined(g0, 0)

                def group(g, left):
                    for r in range(LINES):
                        if r == 0 and left >= 1:
                            energies(g.after(1))
                        if r < 2:
                            column_sums(g, r + 2)
                        elif left >= 1:
                            column_sums(g.after(1), r - 2)
                        if r < 3:
                            transpose_joined(g, r + 1)
                        elif left >= 1:
                            transpose_joined(g.after(1), 0)
                        if r == 1 and left >= 1:
                            transpose_probs(g.after(1))
                        if more and r >= 2 * left:
                            rows_lead(b + 1, r + 2 - left * LINES)
                        project_v(g, r)

                loop_groups(pe, b, True, group)

            for step in range(6):
                rows_lead(0, step)
            loop_images(pe, rows, cols)


def kernel(**inputs):
    import concourse.bacc as bacc
    import numpy as np
    from concourse.bass_utils import run_bass_kernel_spmd

    x = np.asarray(inputs["x"])
    wq, wk, wv = (np.asarray(inputs[f"L0_conv_W{n}"]) for n in "qkv")
    bq, bk, bv = (np.asarray(inputs[f"L0_conv_b{n}"]) for n in "qkv")
    arrays = {
        "x_rows": x.reshape(B, CK, P, NG, GP).transpose(0, 3, 2, 1, 4).reshape(B * NG, P, TILE),
        "x_cols": x.reshape(B, C, H, NG, LINES).transpose(0, 3, 2, 4, 1).reshape(B * NG, P, TILE),
        "w_qk": np.concatenate([wq, wk]).reshape(P, CK, P).transpose(2, 1, 0).reshape(P, CK * P),
        "w_v": wv.reshape(C, CK, P).transpose(2, 1, 0).reshape(P, CK * C),
        "b_qk": np.concatenate([bq, bk]).reshape(P, 1),
        "b_v": bv.reshape(1, C),
        "gamma": np.asarray(inputs["L0_conv_gamma"]).reshape(1, 1),
    }
    arrays = {n: np.ascontiguousarray(a) for n, a in arrays.items()}
    nc = bacc.Bacc("TRN2", target_bir_lowering=False, num_devices=1)
    args = [nc.dram_tensor(n, a.shape, F32, kind="ExternalInput").ap() for n, a in arrays.items()]
    scratch = nc.dram_tensor("row_sums", (B, H, W * C + PAD), F32, kind="Internal").ap()
    out = nc.dram_tensor("out", (B * NG, P, TILE), F32, kind="ExternalOutput").ap()
    criss_cross(nc, *args, scratch, out)
    y = run_bass_kernel_spmd(nc, [arrays], core_ids=[0]).results[0]["out"]
    return np.ascontiguousarray(y.reshape(B, NG, H, LINES, C).transpose(0, 4, 2, 1, 3).reshape(B, C, H, W))
```

```python
from contextlib import ExitStack

import concourse.bass as bass
from concourse import mybir

F32 = mybir.dt.float32
F32R = mybir.dt.float32r
BF16 = mybir.dt.bfloat16
ALU = mybir.AluOpType
ACT = mybir.ActivationFunctionType
AX_X = mybir.AxisListType.X

P = 128
B, C, H, W = 4, 512, 128, 128
CQ = C // 8
CK = C // P
LINES = 4
NG = H // LINES
TILE = LINES * C
GP = LINES * P
PAD = 1024
RROWS = 4
RCOLS = 2
MASK = -(2.0 ** 127)

CR_CHUNK = 4
CR_QK = 2
CR_ONE = 1
CR_Z = 8
CR_T = 2
CR_ZW = 2
CR_Y = 4
CR_ST = 16


def criss_cross(nc, x_rows, x_cols, w_qk, w_v, b_qk, b_v, gamma, scratch, out):
    ctx = ExitStack()
    with ctx:
        def sb(name, shape, dt=F32):
            return ctx.enter_context(nc.sbuf_tensor(name, shape, dt))

        def pb(name, shape, dt=F32):
            return ctx.enter_context(nc.psum_tensor(name, shape, dt))

        def sem(name):
            return ctx.enter_context(nc.semaphore(name))

        def f32(ap):
            return ap.bitcast(F32)

        def lines(ap):
            return ap.rearrange("p (r n) -> p r n", r=LINES)

        tiles = sb("tiles", [P, 4, TILE])
        x_hi = sb("x_hi", [P, CK, GP], F32R)
        x_lo = sb("x_lo", [P, CK, GP], F32R)
        qk = sb("qk", [P, H * W])
        q2 = sb("q2", [P, GP], F32R)
        k_hi2 = sb("k_hi2", [P, GP], F32R)
        k_lo0 = sb("k_lo0", [P, GP], F32R)
        shifted = sb("shifted", [P, GP])
        probs = sb("probs", [P, GP])
        pt_hi = sb("pt_hi", [P, 2, GP], F32R)
        pt_lo = sb("pt_lo", [P, 2, GP], F32R)
        t_hi = sb("t_hi", [P, 2, C], F32R)
        t_lo = sb("t_lo", [P, 2, C], F32R)
        xc_hi = sb("xc_hi", [P, 2, C], F32R)
        xc_lo = sb("xc_lo", [P, 2, C], F32R)
        xb = sb("xb", [P, CR_Y, C])
        joined = sb("joined", [P, 2, C])
        ost = sb("ost", [P, 2, TILE])
        wqk_hi = sb("wqk_hi", [P, CK, P], F32R)
        wqk_lo = sb("wqk_lo", [P, CK, P], F32R)
        wv_hi = sb("wv_hi", [P, CK, C], F32R)
        wv_lo = sb("wv_lo", [P, CK, C], F32R)
        gbv = sb("gbv", [P, C])
        bqk = sb("bqk", [P, 1])
        gam = sb("gam", [P, 1])
        ident = sb("ident", [P, P])
        ident_b = sb("ident_b", [P, P], BF16)
        mask_b = sb("mask_b", [P, GP], BF16)
        row_max = sb("row_max", [P, H])
        row_sum = sb("row_sum", [P, H])
        row_max_t = sb("row_max_t", [P, W])
        row_sum_t = sb("row_sum_t", [P, W])
        col_max = sb("col_max", [P, LINES])
        both_max = sb("both_max", [P, LINES])
        row_shift = sb("row_shift", [P, LINES])
        row_fac = sb("row_fac", [P, 2, LINES])
        sum_a = sb("sum_a", [P, LINES])
        sum_b = sb("sum_b", [P, LINES])
        sum_c = sb("sum_c", [P, LINES])
        sum_r = sb("sum_r", [P, LINES])
        scale = sb("scale", [P, 2, LINES])

        ps_y = [pb(f"ps_y{i}", [P, 512]) for i in range(2)]
        ps_t = [pb(f"ps_t{i}", [P, 512]) for i in range(2)]
        ps_z = [pb(f"ps_z{i}", [P, 512]) for i in range(2)]
        ps_e = pb("ps_e", [P, GP])
        ps_p = pb("ps_p", [P, GP])

        w_in = sem("w_in")
        b_in = sem("b_in")
        wv_in = sem("wv_in")
        x_in = [sem(f"x_in{i}") for i in range(4)]
        xc_in = [sem(f"xc_in{i}") for i in range(2)]
        zw_in = [sem(f"zw_in{i}") for i in range(2)]
        last_in = sem("last_in")
        stored = [sem(f"stored{i}") for i in range(2)]
        tail_stored = sem("tail_stored")
        ident_ok = sem("ident_ok")
        wsplit = sem("wsplit")
        gbv_ok = sem("gbv_ok")
        wv_split = sem("wv_split")
        xh_ok = sem("xh_ok")
        xh2_ok = sem("xh2_ok")
        xl_ok = sem("xl_ok")
        qk_mm = sem("qk_mm")
        qk_kept = sem("qk_kept")
        qk_split_hi = sem("qk_split_hi")
        qk_split = sem("qk_split")
        e_mm = sem("e_mm")
        max_ok = sem("max_ok")
        shift_ok = sem("shift_ok")
        exp_ok = sem("exp_ok")
        sum_ok = sem("sum_ok")
        p_mm = sem("p_mm")
        pth_ok = sem("pth_ok")
        ptl_ok = sem("ptl_ok")
        t_mm = sem("t_mm")
        th_ok = sem("th_ok")
        tl_ok = sem("tl_ok")
        z_mm = sem("z_mm")
        zw_ok = sem("zw_ok")
        stat_mm = sem("stat_mm")
        stat_ok = sem("stat_ok")
        small = sem("small")
        rfac_ok = sem("rfac_ok")
        xch_ok = sem("xch_ok")
        xcl_ok = sem("xcl_ok")
        xb_ok = sem("xb_ok")
        joined_ok = sem("joined_ok")
        y_mm = sem("y_mm")
        y_ok = sem("y_ok")
        SMALL = 6

        block = ctx.enter_context(nc.Block())

        class Group:

            def __init__(self, b, t, j, cols=False):
                ring = RCOLS if cols else RROWS
                self.b, self.cols = b, cols
                self.t, self.slot = t + j // ring, j % ring
                self.g = self.t * ring + self.slot
                self.n = b * NG + self.g
                self.q = b * (2 * NG) + self.g + cols * NG
                self.s = self.slot % 2
                self.pair = b * NG + (self.t + NG // 2 if cols else self.t * 2 + self.slot // 2)
                self.loads = b * (NG // ring) + self.t + 1

            def after(self, k):
                ring = RCOLS if self.cols else RROWS
                return Group(self.b, self.t, self.slot + k, self.cols) if self.slot + k < ring else \
                    Group(self.b, self.t + (self.slot + k) // ring, (self.slot + k) % ring, self.cols)

            def line(self, r):
                return self.n * LINES + r

            def all_line(self, r):
                return self.q * LINES + r

        def loop_groups(eng, b, cols, body):
            ring = RCOLS if cols else RROWS
            turns = NG // ring
            with eng.Fori(0, turns - 1) as t:
                for j in range(ring):
                    body(Group(b, t, j, cols), NG)
            for j in range(ring):
                body(Group(b, turns - 1, j, cols), ring - 1 - j)

        def follows(g, left, k):
            return g.after(k) if left >= k else Group(g.b, 0, k - left - 1, True)

        def loop_images(eng, rows, cols):
            with eng.Fori(0, B - 1) as b:
                rows(b)
                cols(b, True)
            rows(B - 1)
            cols(B - 1, False)

        @block.sync
        def _(sp):
            for s in range(2):
                sp.sem_inc(stored[s], CR_ST)

            def load_rows(g):
                sp.dma_start(tiles[:, g.slot, :], x_rows[bass.ds(g.n, 1), :, :]
                             .rearrange("a p n -> p (a n)")).then_inc(x_in[g.slot], 16)

            def load_cols(g):
                sp.dma_start(tiles[:, 2 * g.s, :], x_cols[bass.ds(g.n, 1), :, :]
                             .rearrange("a p n -> p (a n)")).then_inc(xc_in[g.s], 16)

            def load_sums(g, rows_past=H):
                sp.dma_start(tiles[0:rows_past, 2 * g.s + 1, :],
                             scratch[bass.ds(g.b, 1), 0:rows_past, bass.ds(PAD + g.g * TILE, TILE)]
                             .rearrange("a p n -> p (a n)")).then_inc(zw_in[g.s], 16)

            def store_output(g, first, past, landed):
                sp.dma_start(out[bass.ds(g.n, 1), :, first * C:past * C].rearrange("a p n -> p (a n)"),
                             ost[:, g.s, first * C:past * C]).then_inc(landed, 16)

            def rows(b):
                def group(g, left):
                    if left >= RROWS:
                        sp.wait_ge(t_mm, g.all_line(LINES))
                        load_rows(g.after(RROWS))
                    elif g.s == 0:
                        sp.wait_ge(t_mm, g.all_line(LINES))
                        load_cols(Group(b, 0, g.slot // 2, True))
                    if left == 0:
                        sp.wait_ge(stored[1], (b * NG + NG // 2 - 1) * 16 + CR_ST)
                        sp.wait_ge(stored[0], (b * NG + NG // 2) * 16 + CR_ST)
                        load_sums(Group(b, 0, 0, True), H - LINES)
                        for r in range(LINES):
                            sp.wait_ge(zw_ok, g.line(r + 1) + CR_ZW)
                            sp.dma_start(tiles[H - LINES + r:H - LINES + r + 1, 1, :],
                                         ost[0:LINES, g.s, r * C:(r + 1) * C]).then_inc(last_in, 16)
                    sp.wait_ge(zw_ok, g.line(LINES) + CR_ZW)
                    sp.dma_start(scratch[bass.ds(b, 1), bass.ds(g.g * LINES, LINES), PAD:PAD + W * C]
                                 .rearrange("a h (w c) -> w (a h) c", c=C),
                                 lines(ost[:, g.s, :])).then_inc(stored[g.s], 16)

                loop_groups(sp, b, False, group)

            def cols(b, more):
                sp.wait_ge(stored[1], (b * NG + NG // 2) * 16 + CR_ST)
                load_sums(Group(b, 0, 1, True))

                def group(g, left):
                    if left >= RCOLS or more:
                        sp.wait_ge(xb_ok, g.line(LINES))
                        if left >= RCOLS:
                            load_cols(g.after(RCOLS))
                        else:
                            load_rows(Group(b + 1, 0, 2 * g.s))
                        sp.wait_ge(joined_ok, g.line(LINES))
                        if left >= RCOLS:
                            load_sums(g.after(RCOLS))
                        else:
                            load_rows(Group(b + 1, 0, 2 * g.s + 1))
                    first = 0
                    if left == 0 and not more:
                        first = LINES - 1
                        sp.wait_ge(y_ok, g.line(first) + CR_Y)
                        store_output(g, 0, first, tail_stored)
                    sp.wait_ge(y_ok, g.line(LINES) + CR_Y)
                    store_output(g, first, LINES, stored[g.s])

                loop_groups(sp, b, True, group)

            sp.dma_start(ost[:, 1, 0:CK * P], w_qk).then_inc(w_in, 16)
            load_rows(Group(0, 0, 0))
            sp.dma_start(bqk[:, :], b_qk).then_inc(b_in, 16)
            sp.dma_start(gam[:, :], gamma.to_broadcast([P, 1])).then_inc(b_in, 16)
            sp.dma_start(gbv[:, :], b_v.to_broadcast([P, C])).then_inc(b_in, 16)
            sp.dma_start(ost[:, 0, :], w_v).then_inc(wv_in, 16)
            load_rows(Group(0, 0, 1))
            load_rows(Group(0, 0, 2))
            load_rows(Group(0, 0, 3))
            loop_images(sp, rows, cols)
            for s in range(2):
                sp.wait_ge(stored[s], B * NG * 16 + CR_ST)
            sp.wait_ge(tail_stored, 16)

        @block.gpsimd
        def _(pool):
            nc.gpsimd.memset(ident[:, :], 0.0).then_inc(ident_ok, 1)
            nc.gpsimd.memset(ident_b[:, :], 0.0).then_inc(ident_ok, 1)
            nc.gpsimd.memset(mask_b[:, :], 0.0).then_inc(ident_ok, 1)
            pool.wait_ge(ident_ok, 3)
            for m in (ident, ident_b):
                nc.gpsimd.affine_select(out=m[:, :], in_=m[:, :], compare_op=ALU.not_equal, fill=1.0,
                                        base=0, pattern=[[-1, P]], channel_multiplier=1).then_inc(ident_ok, 1)
            nc.gpsimd.affine_select(out=lines(mask_b[:, :]), in_=lines(mask_b[:, :]), compare_op=ALU.not_equal,
                                    fill=MASK, base=0, pattern=[[0, LINES], [-1, P]],
                                    channel_multiplier=1).then_inc(ident_ok, 1)

            def x_low(g, ck):
                if ck == 2:
                    pool.wait_ge(xh2_ok, g.n + 1)
                else:
                    pool.wait_ge(xh_ok, g.n * (CK - 1) + (3 if ck == 3 else ck + 1))
                nc.gpsimd.tensor_tensor(x_lo[:, ck, :], tiles[:, g.slot, ck * GP:(ck + 1) * GP],
                                        f32(x_hi[:, ck, :]), ALU.subtract).then_inc(xl_ok, 1)

            def rows(b):
                def group(g, left):
                    if left >= 1:
                        for ck in range(CK):
                            x_low(g.after(1), ck)

                loop_groups(pool, b, False, group)

            def cols(b, more):
                def group(g, left):
                    for r in range(LINES):
                        x_line = tiles[:, 2 * g.s, r * C:(r + 1) * C]
                        pool.wait_ge(xch_ok, g.line(r + 1))
                        nc.gpsimd.tensor_tensor(xc_lo[:, r % 2, :], x_line, f32(xc_hi[:, r % 2, :]),
                                                ALU.subtract).then_inc(xcl_ok, 1)
                        pool.wait_ge(y_ok, g.line(r + 1) - CR_Y + CR_Y)
                        nc.gpsimd.tensor_tensor(xb[:, r, :], x_line, gbv[:, :], ALU.add).then_inc(xb_ok, 1)
                    if left == 0 and more:
                        for ck in range(CK):
                            x_low(Group(b + 1, 0, 0), ck)

                loop_groups(pool, b, True, group)

            for ck in range(CK):
                x_low(Group(0, 0, 0), ck)
            pool.wait_ge(gbv_ok, 1)
            loop_images(pool, rows, cols)

        @block.scalar
        def _(act):
            act.sem_inc(qk_kept, CR_QK)
            act.sem_inc(exp_ok, CR_ONE)
            act.sem_inc(zw_ok, CR_ZW)

            def x_high(g, ck):
                if ck == 0:
                    act.wait_ge(x_in[g.slot], g.loads * 16)
                act.wait_ge(qk_mm, g.n * CK + ck + 1 - CR_CHUNK + CR_CHUNK)
                nc.scalar.activation(x_hi[:, ck, :], tiles[:, g.slot, ck * GP:(ck + 1) * GP],
                                     ACT.Copy).then_inc(xh_ok, 1)

            def keep_qk(g, first=False):
                act.wait_ge(qk_mm, (g.n + 1) * CK + CR_CHUNK)
                bank = ps_p if first else ps_y[1 - g.s]
                nc.scalar.activation(qk[:, bass.ds(g.g * GP, GP)], bank[:, :], ACT.Identity,
                                     bias=bqk[:, 0:1]).then_inc(qk_kept, 1)

            def t_high(g, r):
                act.wait_ge(t_mm, g.all_line(r + 1))
                nc.scalar.activation(t_hi[:, r % 2, :], ps_t[r % 2][:, :], ACT.Copy).then_inc(th_ok, 1)

            def exps(g):
                act.wait_ge(shift_ok, g.q + 1 + CR_ONE)
                act.wait_ge(p_mm, g.q + CR_ONE)
                nc.scalar.activation(probs[:, :], shifted[:, :], ACT.Exp).then_inc(exp_ok, 1)

            def pt_high(g):
                act.wait_ge(p_mm, g.q + 1 + CR_ONE)
                act.wait_ge(z_mm, g.all_line(0) - LINES + CR_Z)
                nc.scalar.activation(pt_hi[:, g.s, :], ps_p[:, :], ACT.Copy).then_inc(pth_ok, 1)

            def xc_high(g, r, first=False):
                if r == 0:
                    act.wait_ge(xc_in[g.s], g.loads * 16)
                if not first:
                    act.wait_ge(z_mm, g.all_line(r) - 1 + CR_Z)
                nc.scalar.activation(xc_hi[:, r % 2, :], tiles[:, 2 * g.s, r * C:(r + 1) * C],
                                     ACT.Copy).then_inc(xch_ok, 1)

            def row_factor(g):
                act.wait_ge(small, g.n * SMALL + 2)
                nc.scalar.activation(row_fac[:, g.s, :], row_shift[:, :], ACT.Exp).then_inc(rfac_ok, 1)

            def rows_lead(b, step):
                g0, g1, g2 = (Group(b, 0, j) for j in range(3))
                if step == 0:
                    x_high(g0, 0)
                if step == 1:
                    x_high(g0, 1)
                if step == 2:
                    x_high(g0, 3)
                if step == 4:
                    x_high(g1, 0)
                    x_high(g1, 1)
                    keep_qk(g0, True)
                if step == 5:
                    t_high(g0, 0)
                    x_high(g1, 3)
                    exps(g0)
                if step == 6:
                    t_high(g0, 1)
                    x_high(g2, 0)
                    pt_high(g0)
                    x_high(g2, 1)
                    keep_qk(g1)
                    x_high(g2, 3)

            def rows(b):
                def keep_sums(g, r):
                    if r == 0:
                        act.wait_ge(stored[g.s], g.pair * 16 + CR_ST)
                    act.wait_ge(z_mm, g.all_line(r + 1) + CR_Z)
                    nc.scalar.activation(ost[:, g.s, r * C:(r + 1) * C], ps_z[r % 2][:, :],
                                         ACT.Copy).then_inc(zw_ok, 1)

                def group(g, left):
                    for r in range(LINES):
                        if r != 2:
                            keep_sums(g, r)
                        if r < 2:
                            t_high(g, r + 2)
                        if r == 1 and left == 0:
                            pt_high(follows(g, left, 1))
                        if r == (1 if left else 0):
                            exps(follows(g, left, 1))
                            if left == 0:
                                row_factor(follows(g, left, 1))
                        if r == 1 and left >= 2:
                            keep_qk(g.after(2))
                        if r == 2 and left >= 1:
                            pt_high(g.after(1))
                        if r >= 2 and left >= 1:
                            t_high(g.after(1), r - 2)
                        if r == 2:
                            keep_sums(g, r)
                        if left >= 3 and r != 2:
                            x_high(g.after(3), r)
                        if r >= 2 and left == 1:
                            xc_high(follows(g, left, 2), r - 2, True)

                rows_lead(b, 6)
                loop_groups(act, b, False, group)

            def cols(b, more):
                g0 = Group(b, 0, 0, True)
                xc_high(g0, 2)
                t_high(g0, 0)

                def group(g, left):
                    for r in range(LINES):
                        if r == 0:
                            xc_high(g, 3)
                        elif left >= 1:
                            xc_high(g.after(1), r - 1)
                        if r < 3:
                            t_high(g, r + 1)
                        elif left >= 1:
                            t_high(g.after(1), 0)
                        if r == 0 and left >= 1:
                            exps(g.after(1))
                            row_factor(g.after(1))
                        if r == 1 and left >= 1:
                            pt_high(g.after(1))
                        if more and r >= 2 * left:
                            rows_lead(b + 1, r + 2 - left * LINES)

                loop_groups(act, b, True, group)

            for step in range(6):
                if step == 4:
                    act.wait_ge(b_in, 3 * 16)
                rows_lead(0, step)
            act.wait_ge(wv_split, 2)
            loop_images(act, rows, cols)

        @block.vector
        def _(dve):
            dve.sem_inc(shift_ok, CR_ONE)
            dve.sem_inc(ptl_ok, CR_ONE)
            dve.sem_inc(tl_ok, CR_T)
            dve.sem_inc(y_ok, CR_Y)
            dve.wait_ge(w_in, 16)
            w_qk_in = ost[:, 1, 0:CK * P].rearrange("p (k n) -> p k n", k=CK)
            nc.vector.tensor_copy(wqk_hi[:, :, :], w_qk_in).then_inc(wsplit, 1)
            nc.vector.memset(f32(k_lo0[CQ:P, :]), 0.0).then_inc(wsplit, 1)
            dve.wait_ge(wsplit, 1)
            nc.vector.tensor_tensor(wqk_lo[:, :, :], w_qk_in, f32(wqk_hi[:, :, :]), ALU.subtract).then_inc(wsplit, 1)

            def value_weights():
                dve.wait_ge(b_in, 3 * 16)
                nc.vector.tensor_scalar(gbv[:, :], gbv[:, :], gam[:, 0:1], None, ALU.mult).then_inc(gbv_ok, 1)
                dve.wait_ge(wv_in, 16)
                w_v_in = ost[:, 0, :].rearrange("p (k n) -> p k n", k=CK)
                nc.vector.tensor_copy(wv_hi[:, :, :], w_v_in).then_inc(wv_split, 1)
                dve.wait_ge(wv_split, 1)
                nc.vector.tensor_tensor(wv_lo[:, :, :], w_v_in, f32(wv_hi[:, :, :]), ALU.subtract).then_inc(wv_split, 1)

            def qk_lines(g):
                if g.cols:
                    v = qk[:, :].rearrange("p (h w) -> p w h", w=W)[:, bass.ds(g.g * LINES, LINES), :]
                else:
                    v = lines(qk[:, bass.ds(g.g * GP, GP)])
                return v[0:CQ], v[CQ:P]

            def split_high(g):
                if not g.cols:
                    dve.wait_ge(qk_kept, g.n + 1 + CR_QK)
                dve.wait_ge(e_mm, g.q + CR_ONE)
                q, k = qk_lines(g)
                nc.vector.tensor_copy(lines(q2[0:CQ, :]), q).then_inc(qk_split_hi, 1)
                nc.vector.tensor_copy(lines(k_hi2[CQ:P, :]), k).then_inc(qk_split_hi, 1)
                nc.vector.tensor_copy(lines(k_hi2[0:CQ, :]), k).then_inc(qk_split_hi, 1)

            def split_low(g):
                dve.wait_ge(qk_split_hi, 3 * g.q + 3)
                q, k = qk_lines(g)
                nc.vector.tensor_tensor(lines(q2[CQ:P, :]), q, lines(f32(q2[0:CQ, :])), ALU.subtract).then_inc(qk_split, 1)
                nc.vector.tensor_tensor(lines(k_lo0[0:CQ, :]), k, lines(f32(k_hi2[CQ:P, :])), ALU.subtract).then_inc(qk_split, 1)

            def spread(ap):
                return ap.unsqueeze(2).to_broadcast([P, LINES, P])

            def top_energy(g):
                dve.wait_ge(e_mm, g.q + 1 + CR_ONE)
                top = col_max[:, :] if g.cols else row_max[:, bass.ds(g.g * LINES, LINES)]
                nc.vector.reduce_max(top, lines(ps_e[:, :]), AX_X).then_inc(max_ok, 1)

            def joint_top(g):
                dve.wait_ge(max_ok, g.q + 1)
                nc.vector.tensor_tensor(both_max[:, :], col_max[:, :],
                                        row_max_t[:, bass.ds(g.g * LINES, LINES)], ALU.max).then_inc(small, 1)

            def shift(g):
                if g.cols:
                    dve.wait_ge(small, g.n * SMALL + 1)
                    top = both_max[:, :]
                else:
                    dve.wait_ge(max_ok, g.q + 1)
                    top = row_max[:, bass.ds(g.g * LINES, LINES)]
                dve.wait_ge(exp_ok, g.q + CR_ONE)
                nc.vector.tensor_tensor(lines(shifted[:, :]), lines(ps_e[:, :]), spread(top),
                                        ALU.subtract).then_inc(shift_ok, 1)

            def row_below(g):
                nc.vector.tensor_tensor(row_shift[:, :], row_max_t[:, bass.ds(g.g * LINES, LINES)],
                                        both_max[:, :], ALU.subtract).then_inc(small, 1)

            def total(g):
                dve.wait_ge(exp_ok, g.q + 1 + CR_ONE)
                sums = sum_a[:, :] if g.cols else row_sum[:, bass.ds(g.g * LINES, LINES)]
                nc.vector.reduce_sum(sums, lines(probs[:, :]), AX_X).then_inc(sum_ok, 1)

            def row_total(g):
                dve.wait_ge(rfac_ok, g.n + 1)
                nc.vector.tensor_tensor(sum_b[:, :], row_sum_t[:, bass.ds(g.g * LINES, LINES)],
                                        row_fac[:, g.s, :], ALU.mult).then_inc(small, 1)

            def both_totals(g):
                dve.wait_ge(sum_ok, g.q + 1)
                dve.wait_ge(small, g.n * SMALL + 3)
                nc.vector.tensor_tensor(sum_c[:, :], sum_a[:, :], sum_b[:, :], ALU.add).then_inc(small, 1)

            def inverse(g):
                dve.wait_ge(small, g.n * SMALL + 4)
                nc.vector.reciprocal(sum_r[:, :], sum_c[:, :]).then_inc(small, 1)

            def scales(g):
                dve.wait_ge(small, g.n * SMALL + 5)
                nc.vector.tensor_scalar(scale[:, g.s, :], sum_r[:, :], gam[:, 0:1], None, ALU.mult).then_inc(small, 1)

            def pt_low(g):
                dve.wait_ge(pth_ok, g.q + 1)
                nc.vector.tensor_tensor(pt_lo[:, g.s, :], ps_p[:, :], f32(pt_hi[:, g.s, :]),
                                        ALU.subtract).then_inc(ptl_ok, 1)

            def t_low(g, r):
                dve.wait_ge(th_ok, g.all_line(r + 1))
                nc.vector.tensor_tensor(t_lo[:, r % 2, :], ps_t[r % 2][:, :], f32(t_hi[:, r % 2, :]),
                                        ALU.subtract).then_inc(tl_ok, 1)

            def x_high(g):
                dve.wait_ge(x_in[g.slot], g.loads * 16)
                dve.wait_ge(qk_mm, g.n * CK + 3 - CR_CHUNK + CR_CHUNK)
                nc.vector.tensor_copy(x_hi[:, 2, :], tiles[:, g.slot, 2 * GP:3 * GP]).then_inc(xh2_ok, 1)

            def rows_lead(b, step):
                g0, g1, g2 = (Group(b, 0, j) for j in range(3))
                if step == 2:
                    x_high(g0)
                if step == 4:
                    split_high(g0)
                    split_low(g0)
                if step == 5:
                    x_high(g1)
                    t_low(g0, 0)
                    top_energy(g0)
                    shift(g0)
                if step == 6:
                    t_low(g0, 1)
                    total(g0)
                    pt_low(g0)
                    split_high(g1)
                    x_high(g2)
                    split_low(g1)

            def rows(b):
                def group(g, left):
                    for r in range(LINES):
                        if r == 1 and left >= 1:
                            top_energy(g.after(1))
                            shift(g.after(1))
                        if r == 1 and left >= 3:
                            x_high(g.after(3))
                        if r == 0 and left == 0:
                            c0 = follows(g, left, 1)
                            top_energy(c0)
                            dve.wait_ge(stat_mm, b + 1)
                            nc.vector.tensor_copy(row_max_t[:, :], ps_y[0][:, 0:P]).then_inc(stat_ok, 1)
                            nc.vector.tensor_copy(row_sum_t[:, :], ps_y[0][:, P:2 * P]).then_inc(stat_ok, 1)
                            dve.wait_ge(stat_ok, 2 * b + 2)
                            joint_top(c0)
                            shift(c0)
                            row_below(c0)
                        if r == (2 if left else 1):
                            split_high(follows(g, left, 2))
                        if r == 2 and left == 1:
                            total(g.after(1))
                        if r == 2 and left >= 1:
                            pt_low(g.after(1))
                        if (r == 3 and left >= 2) or (r == 2 and left < 2):
                            split_low(follows(g, left, 2))
                        if r < 2:
                            t_low(g, r + 2)
                        elif left >= 1:
                            t_low(g.after(1), r - 2)
                        if r == 1 and left == 0:
                            pt_low(follows(g, left, 1))
                        if r == 3 and left != 1:
                            total(follows(g, left, 1))

                rows_lead(b, 6)
                loop_groups(dve, b, False, group)

            def cols(b, more):
                def join(g, r, first=False):
                    if r == 0:
                        dve.wait_ge(zw_in[g.s], g.loads * 16)
                        if first:
                            dve.wait_ge(last_in, (b + 1) * LINES * 16)
                    dve.wait_ge(z_mm, g.all_line(r + 1) + CR_Z)
                    nc.vector.scalar_tensor_tensor(out=joined[:, r % 2, :], in0=tiles[:, 2 * g.s + 1, r * C:(r + 1) * C],
                                                   scalar=row_fac[:, g.s, r:r + 1], in1=ps_z[r % 2][:, :],
                                                   op0=ALU.mult, op1=ALU.add).then_inc(joined_ok, 1)

                def output(g, r):
                    if r == 0:
                        dve.wait_ge(stored[g.s], g.pair * 16 + CR_ST)
                        dve.wait_ge(small, g.n * SMALL + SMALL)
                    dve.wait_ge(xb_ok, g.line(r + 1))
                    dve.wait_ge(y_mm, g.line(r + 1))
                    nc.vector.scalar_tensor_tensor(out=ost[:, g.s, r * C:(r + 1) * C], in0=ps_y[r % 2][:, :],
                                                   scalar=scale[:, g.s, r:r + 1], in1=xb[:, r, :],
                                                   op0=ALU.mult, op1=ALU.add).then_inc(y_ok, 1)

                g0 = Group(b, 0, 0, True)
                row_total(g0)
                both_totals(g0)
                inverse(g0)
                scales(g0)
                join(g0, 0, True)
                join(g0, 1)
                t_low(g0, 0)

                def group(g, left):
                    for r in range(LINES):
                        last = left < 1
                        if r == 0 and not last:
                            top_energy(g.after(1))
                        if r < 2:
                            join(g, r + 2)
                        elif not last:
                            join(g.after(1), r - 2)
                        if r == 0 and not last:
                            joint_top(g.after(1))
                            shift(g.after(1))
                        if r == 2 and left >= 2:
                            split_low(g.after(2))
                        if r == 3 and not last:
                            both_totals(g.after(1))
                        if r < 3:
                            t_low(g, r + 1)
                        elif not last:
                            t_low(g.after(1), 0)
                        if r == 0 and not last:
                            row_below(g.after(1))
                        if r == 1 and not last:
                            pt_low(g.after(1))
                        if r == 1 and left >= 2:
                            split_high(g.after(2))
                        if r == 2 and not last:
                            total(g.after(1))
                            row_total(g.after(1))
                        if r == 3 and not last:
                            inverse(g.after(1))
                        if more and r >= 2 * left:
                            rows_lead(b + 1, r + 2 - left * LINES)
                        output(g, r)
                        if r == 3 and not last:
                            scales(g.after(1))

                loop_groups(dve, b, True, group)

            for step in range(6):
                rows_lead(0, step)
                if step == 3:
                    value_weights()
            loop_images(dve, rows, cols)

        @block.tensor
        def _(pe):
            pe.sem_inc(qk_mm, CR_CHUNK)
            pe.sem_inc(e_mm, CR_ONE)
            pe.sem_inc(p_mm, CR_ONE)
            pe.sem_inc(z_mm, CR_Z)
            pe.wait_ge(ident_ok, 6)
            pe.wait_ge(wsplit, 3)

            def energies(g):
                pe.wait_ge(qk_split, 2 * g.q + 2)
                pe.wait_ge(shift_ok, g.q + CR_ONE)
                if g.cols:
                    nc.tensor.matmul(ps_e[:, :], ident_b[:, :], mask_b[:, :], start=True, stop=False)
                for r in range(LINES):
                    l = slice(r * P, (r + 1) * P)
                    nc.tensor.matmul(ps_e[:, l], q2[:, l], k_hi2[:, l], start=not g.cols, stop=False)
                    last = nc.tensor.matmul(ps_e[:, l], q2[:, l], k_lo0[:, l], start=False,
                                            stop=not g.cols or r == LINES - 1)
                last.then_inc(e_mm, 1)

            def transpose_probs(g):
                pe.wait_ge(exp_ok, g.q + 1 + CR_ONE)
                pe.wait_ge(ptl_ok, g.q + CR_ONE)
                for r in range(LINES):
                    l = slice(r * P, (r + 1) * P)
                    last = nc.tensor.transpose(ps_p[:, l], probs[:, l], ident[:, :])
                last.then_inc(p_mm, 1)

            def transpose_line(g, r, src):
                pe.wait_ge(tl_ok, g.all_line(r) - 1 + CR_T)
                for ck in range(CK):
                    last = nc.tensor.transpose(ps_t[r % 2][:, ck * P:(ck + 1) * P], src(ck), ident[:, :])
                last.then_inc(t_mm, 1)

            def sums(g, r, hi, lo):
                if r == 0:
                    pe.wait_ge(ptl_ok, g.q + 1 + CR_ONE)
                l = slice(r * P, (r + 1) * P)
                bank, s = ps_z[r % 2][:, :], r % 2
                nc.tensor.matmul(bank, pt_hi[:, g.s, l], hi[:, s, :], start=True, stop=False)
                nc.tensor.matmul(bank, pt_lo[:, g.s, l], hi[:, s, :], start=False, stop=False)
                nc.tensor.matmul(bank, pt_hi[:, g.s, l], lo[:, s, :], start=False, stop=True).then_inc(z_mm, 1)

            def project_qk(g, ck, first=0):
                if ck == 0:
                    if first == 1:
                        pe.wait_ge(ptl_ok, g.q + CR_ONE)
                    elif first:
                        pe.wait_ge(y_ok, g.b * W - (first == 2) + CR_Y)
                    else:
                        pe.wait_ge(qk_kept, g.n - 1 + CR_QK)
                pe.wait_ge(xl_ok, g.n * CK + ck + 1)
                bank = (ps_p if first == 1 else ps_y[1 - g.s])[:, :]
                nc.tensor.matmul(bank, wqk_hi[:, ck, :], x_hi[:, ck, :], start=ck == 0, stop=False)
                nc.tensor.matmul(bank, wqk_lo[:, ck, :], x_hi[:, ck, :], start=False, stop=False)
                nc.tensor.matmul(bank, wqk_hi[:, ck, :], x_lo[:, ck, :], start=False,
                                 stop=ck == CK - 1).then_inc(qk_mm, 1)

            def transpose_x(g, r):
                transpose_line(g, r, lambda ck: tiles[:, g.slot, ck * GP + r * P:ck * GP + (r + 1) * P])

            def rows_lead(b, step):
                g0, g1, g2 = (Group(b, 0, j) for j in range(3))
                if step == 3:
                    project_qk(g0, 0, 1)
                    project_qk(g0, 1, 1)
                if step == 4:
                    project_qk(g0, 2, 1)
                    project_qk(g0, 3, 1)
                if step == 5:
                    transpose_x(g0, 0)
                    energies(g0)
                if step == 6:
                    transpose_x(g0, 1)
                    project_qk(g1, 0, 2)
                    project_qk(g1, 1, 2)
                    transpose_probs(g0)
                    project_qk(g1, 2, 2)
                    project_qk(g1, 3, 2)
                    project_qk(g2, 0, 3)
                    project_qk(g2, 1, 3)

            def rows(b):
                def row_sums(g, r):
                    pe.wait_ge(tl_ok, g.all_line(r + 1) + CR_T)
                    pe.wait_ge(zw_ok, g.line(r) - 1 + CR_ZW)
                    sums(g, r, t_hi, t_lo)

                def group(g, left):
                    for r in range(LINES):
                        if r == 1 and left >= 1:
                            energies(g.after(1))
                        row_sums(g, r)
                        if r == 0 and left == 0:
                            pe.wait_ge(sum_ok, b * 2 * NG + NG)
                            nc.tensor.transpose(ps_y[0][:, 0:P], row_max[:, :], ident[:, :])
                            nc.tensor.transpose(ps_y[0][:, P:2 * P], row_sum[:, :], ident[:, :]).then_inc(stat_mm, 1)
                        if r < 2:
                            transpose_x(g, r + 2)
                        elif left >= 1:
                            transpose_x(g.after(1), r - 2)
                        if r == 3 and left == 1:
                            energies(follows(g, left, 2))
                        if r == (2 if left else 1):
                            transpose_probs(follows(g, left, 1))
                        if r < 2 and left >= 2:
                            project_qk(g.after(2), r + 2)
                        elif r >= 2 and left >= 3:
                            project_qk(g.after(3), r - 2)

                rows_lead(b, 6)
                loop_groups(pe, b, False, group)

            def cols(b, more):
                def column_sums(g, r, first=False):
                    pe.wait_ge(xcl_ok, g.line(r + 1))
                    if first:
                        pe.wait_ge(zw_ok, b * H + H - 1 + r + CR_ZW)
                    else:
                        pe.wait_ge(joined_ok, g.line(r) - 1)
                    sums(g, r, xc_hi, xc_lo)

                def transpose_joined(g, r):
                    pe.wait_ge(joined_ok, g.line(r + 1))
                    transpose_line(g, r, lambda ck: joined[:, r % 2, ck * P:(ck + 1) * P])

                def project_v(g, r):
                    pe.wait_ge(tl_ok, g.all_line(r + 1) + CR_T)
                    pe.wait_ge(y_ok, g.line(r) - 1 + CR_Y)
                    bank, s = ps_y[r % 2][:, :], r % 2
                    for ck in range(CK):
                        l = slice(ck * P, (ck + 1) * P)
                        nc.tensor.matmul(bank, t_hi[:, s, l], wv_hi[:, ck, :], start=ck == 0, stop=False)
                        nc.tensor.matmul(bank, t_hi[:, s, l], wv_lo[:, ck, :], start=False, stop=False)
                        last = nc.tensor.matmul(bank, t_lo[:, s, l], wv_hi[:, ck, :], start=False, stop=ck == CK - 1)
                    last.then_inc(y_mm, 1)

                g0 = Group(b, 0, 0, True)
                column_sums(g0, 0, True)
                column_sums(g0, 1, True)
                energies(Group(b, 0, 1, True))
                transpose_joined(g0, 0)

                def group(g, left):
                    for r in range(LINES):
                        if r < 2:
                            column_sums(g, r + 2)
                        elif left >= 1:
                            column_sums(g.after(1), r - 2)
                        if r == 3 and left >= 2:
                            energies(g.after(2))
                        if r < 3:
                            transpose_joined(g, r + 1)
                        elif left >= 1:
                            transpose_joined(g.after(1), 0)
                        if r == 1 and left >= 1:
                            transpose_probs(g.after(1))
                        if more and r >= 2 * left:
                            rows_lead(b + 1, r + 2 - left * LINES)
                        project_v(g, r)

                loop_groups(pe, b, True, group)

            for step in range(6):
                rows_lead(0, step)
            pe.wait_ge(wv_split, 2)
            loop_images(pe, rows, cols)


def kernel(**inputs):
    import concourse.bacc as bacc
    import numpy as np
    from concourse.bass_utils import run_bass_kernel_spmd

    x = np.asarray(inputs["x"])
    wq, wk, wv = (np.asarray(inputs[f"L0_conv_W{n}"]) for n in "qkv")
    bq, bk, bv = (np.asarray(inputs[f"L0_conv_b{n}"]) for n in "qkv")
    arrays = {
        "x_rows": x.reshape(B, CK, P, NG, GP).transpose(0, 3, 2, 1, 4).reshape(B * NG, P, TILE),
        "x_cols": x.reshape(B, C, H, NG, LINES).transpose(0, 3, 2, 4, 1).reshape(B * NG, P, TILE),
        "w_qk": np.concatenate([wq, wk]).reshape(P, CK, P).transpose(2, 1, 0).reshape(P, CK * P),
        "w_v": wv.reshape(C, CK, P).transpose(2, 1, 0).reshape(P, CK * C),
        "b_qk": np.concatenate([bq, bk]).reshape(P, 1),
        "b_v": bv.reshape(1, C),
        "gamma": np.asarray(inputs["L0_conv_gamma"]).reshape(1, 1),
    }
    arrays = {n: np.ascontiguousarray(a) for n, a in arrays.items()}
    nc = bacc.Bacc("TRN2", target_bir_lowering=False, num_devices=1)
    args = [nc.dram_tensor(n, a.shape, F32, kind="ExternalInput").ap() for n, a in arrays.items()]
    scratch = nc.dram_tensor("row_sums", (B, H, W * C + PAD), F32, kind="Internal").ap()
    out = nc.dram_tensor("out", (B * NG, P, TILE), F32, kind="ExternalOutput").ap()
    criss_cross(nc, *args, scratch, out)
    y = run_bass_kernel_spmd(nc, [arrays], core_ids=[0]).results[0]["out"]
    return np.ascontiguousarray(y.reshape(B, NG, H, LINES, C).transpose(0, 4, 2, 1, 3).reshape(B, C, H, W))
```
